# Optimizing a Trainium2 kernel written in Bass

```python
import numpy as np
import jax
import jax.numpy as jnp

def _softmax(x, axis=-1):
    return jax.nn.softmax(x, axis=axis)

def _gelu(x):
    return jax.nn.gelu(x, approximate=True)

def _silu(x):
    return jax.nn.silu(x)

def _sigmoid(x):
    return jax.nn.sigmoid(x)

def _layernorm(x, axis=-1, eps=1e-05):
    m = jnp.mean(x, axis=axis, keepdims=True)
    v = jnp.var(x, axis=axis, keepdims=True)
    return (x - m) / jnp.sqrt(v + eps)

def _scatter_add(tgt, idx, src, axis=0):
    return tgt.at[idx].add(src)

def _segment_sum(src, seg, n):
    return jax.ops.segment_sum(src, seg, n)
kernel_name = 'mk_vit_tower_cls_d2_tok_img768_r4_c0331a'

def setup_inputs(seed: int=0):
    np.random.seed(seed)
    _w = jnp.asarray

    def _rec_inputs():
        import jax
        import jax.numpy as jnp
        _rk = jax.random.key(seed)
        x = -0.000596345 + 1.00056 * jax.random.normal(jax.random.fold_in(_rk, 1), (4, 3, 64, 64), jnp.float32)
        cls_tok = 0.02 * jax.random.normal(jax.random.fold_in(_rk, 5), (1, 1, 192), jnp.float32)
        return (x, cls_tok)
    x, cls_tok = _rec_inputs()

    def _L0_tok_setup():
        import jax, jax.numpy as jnp
        import numpy as np
        B = 16
        IMG = 64
        CH = 3
        EMBED = 64
        GP = 16
        PRE = [1, 2, 4]
        N_LEVELS = 3
        FUSED = EMBED * N_LEVELS

        def hilbert_flat_indices(n):
            t = np.arange(n * n, dtype=np.int64)
            x = np.zeros(n * n, dtype=np.int64)
            y = np.zeros(n * n, dtype=np.int64)
            s = 1
            while s < n:
                rx = 1 & t // 2
                ry = 1 & (t ^ rx)
                swap = ry == 0
                flip = swap & (rx == 1)
                x = np.where(flip, s - 1 - x, x)
                y = np.where(flip, s - 1 - y, y)
                x2 = np.where(swap, y, x)
                y2 = np.where(swap, x, y)
                x, y = (x2, y2)
                x = x + s * rx
                y = y + s * ry
                t = t // 4
                s *= 2
            return y * n + x

        def _level(x, idx, W, b, p, gp):
            Bsz, C, H, _ = x.shape
            h = H // p
            t = x.reshape(Bsz, C, h, p, h, p).transpose(0, 2, 4, 3, 5, 1).reshape(Bsz, h * h, p * p * C)
            t = t[:, idx]
            t = t.reshape(Bsz, h * h // gp, gp * p * p * C)
            return t @ W.T + b

        def _interp_linear(x, n_out):
            L = x.shape[1]
            pos = (jnp.arange(n_out, dtype=jnp.float32) + 0.5) * (L / n_out) - 0.5
            pos = jnp.clip(pos, 0.0, L - 1)
            i0 = jnp.floor(pos).astype(jnp.int32)
            i1 = jnp.minimum(i0 + 1, L - 1)
            w = (pos - i0).astype(x.dtype)
            return x[:, i0] * (1.0 - w)[None, :, None] + x[:, i1] * w[None, :, None]
        key = jax.random.key(seed)
        ks = jax.random.split(key, 9)
        inp = {'x': jax.random.normal(ks[0], (B, CH, IMG, IMG), jnp.float32)}
        for i, p in enumerate(PRE):
            din = CH * p * p * GP
            inp[f'W{i}'] = jax.random.normal(ks[1 + 2 * i], (EMBED, din), jnp.float32) * din ** (-0.5)
            inp[f'b{i}'] = jax.random.normal(ks[2 + 2 * i], (EMBED,), jnp.float32) * 0.02
        inp['Wf'] = jax.random.normal(ks[7], (FUSED, FUSED), jnp.float32) * FUSED ** (-0.5)
        inp['bf'] = jax.random.normal(ks[8], (FUSED,), jnp.float32) * 0.02
        for i, p in enumerate(PRE):
            inp[f'idx{i}'] = jnp.asarray(hilbert_flat_indices(IMG // p), jnp.int32)
        return inp
    _L0_tok_all = _L0_tok_setup()
    _L0_tok_in = {k: v for k, v in _L0_tok_all.items() if k in ('W0', 'b0', 'W1', 'b1', 'W2', 'b2', 'Wf', 'bf', 'idx0', 'idx1', 'idx2')}
    del _L0_tok_all

    def _L0_attn_setup():
        import jax, jax.numpy as jnp
        import numpy as np
        key = jax.random.key(seed)
        k1, k2, k3, k4, k5 = jax.random.split(key, 5)
        B, N, C = (16, 256, 192)
        x = jax.random.normal(k1, (B, N, C), dtype=jnp.float32)
        sc_token = jax.random.normal(k2, (1, 196, C), dtype=jnp.float32) * 0.02
        W_qkv = jax.random.normal(k3, (C, 3 * C), dtype=jnp.float32) * 0.02
        W_proj = jax.random.normal(k4, (C, C), dtype=jnp.float32) * 0.02
        b_proj = jax.random.normal(k5, (C,), dtype=jnp.float32) * 0.02
        return {'x': x, 'sc_token': sc_token, 'W_qkv': W_qkv, 'W_proj': W_proj, 'b_proj': b_proj}
    _L0_attn_all = _L0_attn_setup()
    _L0_attn_in = {k: v for k, v in _L0_attn_all.items() if k in ('sc_token', 'W_qkv', 'W_proj', 'b_proj')}
    del _L0_attn_all

    def _L0_ffn_setup():
        import jax, jax.numpy as jnp
        import numpy as np
        B, L, D = (4, 256, 192)
        E, S, H = (32, 32, 768)
        EPS = 1e-12

        def _l2norm(v, axis):
            n = jnp.sqrt(jnp.sum(v * v, axis=axis, keepdims=True))
            return v / jnp.maximum(n, EPS)
        key = jax.random.key(seed)
        ks = jax.random.split(key, 6)
        x = jax.random.normal(ks[0], (B, L, D), dtype=jnp.float32)
        phi = jax.random.normal(ks[1], (D, E, S), dtype=jnp.float32) / np.sqrt(D)
        scale = jnp.ones((1,), dtype=jnp.float32)
        w1 = jax.random.normal(ks[2], (E, D, H), dtype=jnp.float32) / np.sqrt(D)
        b1 = jax.random.normal(ks[3], (E, H), dtype=jnp.float32) * 0.01
        w2 = jax.random.normal(ks[4], (E, H, D), dtype=jnp.float32) / np.sqrt(H)
        b2 = jax.random.normal(ks[5], (E, D), dtype=jnp.float32) * 0.01
        return {'x': x, 'phi': phi, 'scale': scale, 'w1': w1, 'b1': b1, 'w2': w2, 'b2': b2}
    _L0_ffn_all = _L0_ffn_setup()
    _L0_ffn_in = {k: v for k, v in _L0_ffn_all.items() if k in ('phi', 'scale', 'w1', 'b1', 'w2', 'b2')}
    del _L0_ffn_all

    def _L1_attn_setup():
        import jax, jax.numpy as jnp
        import numpy as np
        D_MODEL = 192
        NUM_HEADS = 48
        HEAD_CH = D_MODEL // NUM_HEADS
        INNER = 3 * D_MODEL
        BATCH = 2
        SEQLEN = 512
        SKIP = 1.0
        EPS = 1e-06
        key = jax.random.key(seed)
        ks = jax.random.split(key, 9)
        s_in = 1.0 / np.sqrt(D_MODEL)
        s_out = 1.0 / np.sqrt(D_MODEL)
        return {'inputs': jax.random.normal(ks[0], (BATCH, SEQLEN, D_MODEL), jnp.float32), 'w_in': jax.random.normal(ks[1], (INNER, D_MODEL), jnp.float32) * s_in, 'b_in': jax.random.normal(ks[2], (INNER,), jnp.float32) * 0.01, 'w_sf': jax.random.normal(ks[3], (INNER, 3), jnp.float32) * 0.3, 'b_sf': jax.random.normal(ks[4], (INNER,), jnp.float32) * 0.01, 'h': jax.random.normal(ks[5], (NUM_HEADS, SEQLEN), jnp.float32) * 0.02, 'norm_w': jnp.ones((D_MODEL,), jnp.float32), 'w_out': jax.random.normal(ks[6], (D_MODEL, D_MODEL), jnp.float32) * s_out, 'b_out': jax.random.normal(ks[7], (D_MODEL,), jnp.float32) * 0.01}
    _L1_attn_all = _L1_attn_setup()
    _L1_attn_in = {k: v for k, v in _L1_attn_all.items() if k in ('w_in', 'b_in', 'w_sf', 'b_sf', 'h', 'norm_w', 'w_out', 'b_out')}
    del _L1_attn_all

    def _L1_ffn_setup():
        import jax, jax.numpy as jnp
        import numpy as np
        D_MODEL = 192
        D_FF = 768
        NUM_EXPERTS = 8
        EXPERT_CAPACITY = 256
        key = jax.random.key(seed)
        k0, k1, k2, k3 = jax.random.split(key, 4)
        hidden_states = jax.random.normal(k0, (2, 256, D_MODEL), dtype=jnp.float32)
        router_w = jax.random.normal(k1, (D_MODEL, NUM_EXPERTS), dtype=jnp.float32) * D_MODEL ** (-0.5)
        wi = jax.random.normal(k2, (NUM_EXPERTS, D_MODEL, D_FF), dtype=jnp.float32) * D_MODEL ** (-0.5)
        wo = jax.random.normal(k3, (NUM_EXPERTS, D_FF, D_MODEL), dtype=jnp.float32) * D_FF ** (-0.5)
        return {'hidden_states': hidden_states, 'router_w': router_w, 'wi': wi, 'wo': wo}
    _L1_ffn_all = _L1_ffn_setup()
    _L1_ffn_in = {k: v for k, v in _L1_ffn_all.items() if k in ('router_w', 'wi', 'wo')}
    del _L1_ffn_all
    return {'x': x, 'cls_tok': cls_tok, 'L0_tok_W0': _L0_tok_in['W0'], 'L0_tok_b0': _L0_tok_in['b0'], 'L0_tok_W1': _L0_tok_in['W1'], 'L0_tok_b1': _L0_tok_in['b1'], 'L0_tok_W2': _L0_tok_in['W2'], 'L0_tok_b2': _L0_tok_in['b2'], 'L0_tok_Wf': _L0_tok_in['Wf'], 'L0_tok_bf': _L0_tok_in['bf'], 'L0_tok_idx0': _L0_tok_in['idx0'], 'L0_tok_idx1': _L0_tok_in['idx1'], 'L0_tok_idx2': _L0_tok_in['idx2'], 'L0_attn_sc_token': _L0_attn_in['sc_token'], 'L0_attn_W_qkv': _L0_attn_in['W_qkv'], 'L0_attn_W_proj': _L0_attn_in['W_proj'], 'L0_attn_b_proj': _L0_attn_in['b_proj'], 'L0_ffn_phi': _L0_ffn_in['phi'], 'L0_ffn_scale': _L0_ffn_in['scale'], 'L0_ffn_w1': _L0_ffn_in['w1'], 'L0_ffn_b1': _L0_ffn_in['b1'], 'L0_ffn_w2': _L0_ffn_in['w2'], 'L0_ffn_b2': _L0_ffn_in['b2'], 'L1_attn_w_in': _L1_attn_in['w_in'], 'L1_attn_b_in': _L1_attn_in['b_in'], 'L1_attn_w_sf': _L1_attn_in['w_sf'], 'L1_attn_b_sf': _L1_attn_in['b_sf'], 'L1_attn_h': _L1_attn_in['h'], 'L1_attn_norm_w': _L1_attn_in['norm_w'], 'L1_attn_w_out': _L1_attn_in['w_out'], 'L1_attn_b_out': _L1_attn_in['b_out'], 'L1_ffn_router_w': _L1_ffn_in['router_w'], 'L1_ffn_wi': _L1_ffn_in['wi'], 'L1_ffn_wo': _L1_ffn_in['wo']}

def reference(x, cls_tok, L0_tok_W0, L0_tok_b0, L0_tok_W1, L0_tok_b1, L0_tok_W2, L0_tok_b2, L0_tok_Wf, L0_tok_bf, L0_tok_idx0, L0_tok_idx1, L0_tok_idx2, L0_attn_sc_token, L0_attn_W_qkv, L0_attn_W_proj, L0_attn_b_proj, L0_ffn_phi, L0_ffn_scale, L0_ffn_w1, L0_ffn_b1, L0_ffn_w2, L0_ffn_b2, L1_attn_w_in, L1_attn_b_in, L1_attn_w_sf, L1_attn_b_sf, L1_attn_h, L1_attn_norm_w, L1_attn_w_out, L1_attn_b_out, L1_ffn_router_w, L1_ffn_wi, L1_ffn_wo):
    import jax
    import jax.numpy as jnp

    def _L0_tok_ref(x, W0, b0, W1, b1, W2, b2, Wf, bf, idx0, idx1, idx2):
        import jax, jax.numpy as jnp
        import numpy as np
        B = 16
        IMG = 64
        CH = 3
        EMBED = 64
        GP = 16
        PRE = [1, 2, 4]
        N_LEVELS = 3
        FUSED = EMBED * N_LEVELS

        def hilbert_flat_indices(n):
            t = np.arange(n * n, dtype=np.int64)
            x = np.zeros(n * n, dtype=np.int64)
            y = np.zeros(n * n, dtype=np.int64)
            s = 1
            while s < n:
                rx = 1 & t // 2
                ry = 1 & (t ^ rx)
                swap = ry == 0
                flip = swap & (rx == 1)
                x = np.where(flip, s - 1 - x, x)
                y = np.where(flip, s - 1 - y, y)
                x2 = np.where(swap, y, x)
                y2 = np.where(swap, x, y)
                x, y = (x2, y2)
                x = x + s * rx
                y = y + s * ry
                t = t // 4
                s *= 2
            return y * n + x

        def _level(x, idx, W, b, p, gp):
            Bsz, C, H, _ = x.shape
            h = H // p
            t = x.reshape(Bsz, C, h, p, h, p).transpose(0, 2, 4, 3, 5, 1).reshape(Bsz, h * h, p * p * C)
            t = t[:, idx]
            t = t.reshape(Bsz, h * h // gp, gp * p * p * C)
            return t @ W.T + b

        def _interp_linear(x, n_out):
            L = x.shape[1]
            pos = (jnp.arange(n_out, dtype=jnp.float32) + 0.5) * (L / n_out) - 0.5
            pos = jnp.clip(pos, 0.0, L - 1)
            i0 = jnp.floor(pos).astype(jnp.int32)
            i1 = jnp.minimum(i0 + 1, L - 1)
            w = (pos - i0).astype(x.dtype)
            return x[:, i0] * (1.0 - w)[None, :, None] + x[:, i1] * w[None, :, None]
        Ws = [(idx0, W0, b0, PRE[0]), (idx1, W1, b1, PRE[1]), (idx2, W2, b2, PRE[2])]
        outs = [_level(x, idx, W, b, p, GP) for idx, W, b, p in Ws]
        n_tokens = outs[0].shape[1]
        outs = [outs[0]] + [_interp_linear(o, n_tokens) for o in outs[1:]]
        y = jnp.concatenate(outs, axis=-1)
        return y @ Wf.T + bf

    def _L0_attn_ref(x, sc_token, W_qkv, W_proj, b_proj):
        import jax, jax.numpy as jnp
        import numpy as np
        B, N, C = x.shape
        H = 12
        Dh = C // H
        scale = Dh ** (-0.5)
        xt = jnp.concatenate([x, jnp.broadcast_to(sc_token, (B,) + sc_token.shape[1:])], axis=1)
        N1 = xt.shape[1]
        qkv = (xt @ W_qkv).reshape(B, N1, 3, H, Dh)
        q = qkv[:, :, 0].transpose(0, 2, 1, 3)
        k = qkv[:, :, 1].transpose(0, 2, 1, 3)
        v = qkv[:, :, 2].transpose(0, 2, 1, 3)
        attn = jax.nn.softmax(jnp.einsum('bhqd,bhkd->bhqk', q, k) * scale, axis=-1)
        out = jnp.einsum('bhqk,bhkd->bhqd', attn, v)
        out = out.transpose(0, 2, 1, 3).reshape(B, N1, C)
        out = out[:, :N, :]
        return out @ W_proj + b_proj

    def _L0_ffn_ref(x, phi, scale, w1, b1, w2, b2):
        import jax, jax.numpy as jnp
        import numpy as np
        B, L, D = (4, 256, 192)
        E, S, H = (32, 32, 768)
        EPS = 1e-12

        def _l2norm(v, axis):
            n = jnp.sqrt(jnp.sum(v * v, axis=axis, keepdims=True))
            return v / jnp.maximum(n, EPS)
        b, l, d = x.shape
        xn = _l2norm(x, axis=2)
        phin = scale * _l2norm(phi, axis=0)
        logits = jnp.einsum('bld,des->bles', xn, phin)
        d_w = jax.nn.softmax(logits, axis=-1)
        c_w = jax.nn.softmax(logits.reshape(b, l, E * S), axis=-1)
        slots = jnp.einsum('bld,bles->besd', xn, d_w)
        h = jax.nn.gelu(jnp.einsum('besd,edh->besh', slots, w1) + b1[:, None, :], approximate=False)
        eo = jnp.einsum('besh,ehd->besd', h, w2) + b2[:, None, :]
        eo = eo.reshape(b, E * S, d)
        return jnp.einsum('bkd,blk->bld', eo, c_w)

    def _L1_attn_ref(inputs, w_in, b_in, w_sf, b_sf, h, norm_w, w_out, b_out):
        import jax, jax.numpy as jnp
        import numpy as np
        D_MODEL = 192
        NUM_HEADS = 48
        HEAD_CH = D_MODEL // NUM_HEADS
        INNER = 3 * D_MODEL
        BATCH = 2
        SEQLEN = 512
        SKIP = 1.0
        EPS = 1e-06
        B, L, D = inputs.shape
        N, HC = (NUM_HEADS, HEAD_CH)
        u = jnp.einsum('bld,ed->ble', inputs, w_in) + b_in
        u = jnp.transpose(u, (0, 2, 1))
        up = jnp.pad(u, ((0, 0), (0, 0), (2, 0)))
        uc = w_sf[:, 0:1] * up[:, :, 0:L] + w_sf[:, 1:2] * up[:, :, 1:L + 1] + w_sf[:, 2:3] * up[:, :, 2:L + 2] + b_sf[:, None]
        uc = uc.reshape(B, N, 3 * HC, L)
        x0 = uc[:, :, 0:HC, :]
        x1 = uc[:, :, HC:2 * HC, :]
        v = uc[:, :, 2 * HC:3 * HC, :]
        kv = jnp.einsum('bnil,bnjl->bijnl', x1, v)
        fft_size = 2 * L
        k_f = jnp.fft.rfft(h, n=fft_size) / fft_size
        u_f = jnp.fft.rfft(kv, n=fft_size, axis=-1)
        hkv = jnp.fft.irfft(u_f * k_f, n=fft_size, axis=-1, norm='forward')[..., :L]
        qhkv = jnp.einsum('bijnl,bnil->blnj', hkv, x0)
        y = qhkv.reshape(B, L, D)
        ms = jnp.mean(jnp.square(y), axis=-1, keepdims=True)
        y = y * jax.lax.rsqrt(ms + EPS) * norm_w
        y = jnp.einsum('bld,ed->ble', y, w_out) + b_out
        return y + inputs * SKIP

    def _L1_ffn_ref(hidden_states, router_w, wi, wo):
        import jax, jax.numpy as jnp
        import numpy as np
        D_MODEL = 192
        D_FF = 768
        NUM_EXPERTS = 8
        EXPERT_CAPACITY = 256
        B, S, d = hidden_states.shape
        E = router_w.shape[1]
        x = hidden_states.reshape(-1, d)
        logits = x.astype(jnp.float32) @ router_w.astype(jnp.float32)
        probs = jax.nn.softmax(logits, axis=-1).astype(x.dtype)
        p = jnp.max(probs, axis=-1)
        e_idx = jnp.argmax(probs, axis=-1)
        mask = jax.nn.one_hot(e_idx, E, dtype=x.dtype)
        token_priority = jnp.cumsum(mask[:, None, :], axis=-2)[:, 0, :]
        mask = mask * (token_priority <= EXPERT_CAPACITY).astype(x.dtype)
        combine = mask * p[:, None]

        def body(acc, ew):
            Wi_e, Wo_e, w_e = ew
            h = jax.nn.relu(x @ Wi_e) @ Wo_e
            return (acc + w_e[:, None] * h, None)
        out, _ = jax.lax.scan(body, jnp.zeros_like(x), (wi, wo, combine.T))
        return out.reshape(B, S, d)
    h = _L0_tok_ref(x, L0_tok_W0, L0_tok_b0, L0_tok_W1, L0_tok_b1, L0_tok_W2, L0_tok_b2, L0_tok_Wf, L0_tok_bf, L0_tok_idx0, L0_tok_idx1, L0_tok_idx2)
    h = jnp.concatenate([jnp.broadcast_to(cls_tok, (h.shape[0], 1, h.shape[2])), h], axis=1)
    h = h + _L0_attn_ref(_layernorm(h, axis=-1), L0_attn_sc_token, L0_attn_W_qkv, L0_attn_W_proj, L0_attn_b_proj)
    h = h + _L0_ffn_ref(_layernorm(h, axis=-1), L0_ffn_phi, L0_ffn_scale, L0_ffn_w1, L0_ffn_b1, L0_ffn_w2, L0_ffn_b2)
    h = h + _L1_attn_ref(_layernorm(h, axis=-1), L1_attn_w_in, L1_attn_b_in, L1_attn_w_sf, L1_attn_b_sf, L1_attn_h, L1_attn_norm_w, L1_attn_w_out, L1_attn_b_out)
    h = h + _L1_ffn_ref(_layernorm(h, axis=-1), L1_ffn_router_w, L1_ffn_wi, L1_ffn_wo)
    return h

_drawn_inputs = setup_inputs


def setup_inputs(seed=0):
    import zlib

    import numpy as np

    out = dict(_drawn_inputs(seed))
    spreads = {'L1_attn_norm_w': (1.0, 0.2)}
    factors = {'L0_tok_b0': 3.102,
     'L0_tok_b1': 3.128,
     'L0_tok_b2': 2.746,
     'L0_attn_sc_token': 200.0,
     'L0_ffn_phi': 200.0,
     'L0_ffn_b1': 25.436,
     'L0_ffn_b2': 8.0,
     'L1_attn_b_in': 4.528,
     'L1_attn_b_sf': 2.775,
     'L1_attn_b_out': 6.752,
     'L0_attn_W_proj': 2.736}
    for name, (base, spread) in spreads.items():
        noise = np.random.default_rng([zlib.crc32(name.encode()), seed]).standard_normal(out[name].shape)
        drawn = base * np.exp(spread * noise) if base else spread * noise
        out[name] = jnp.asarray(drawn.astype(out[name].dtype))
    for name, factor in factors.items():
        out[name] = (out[name] * factor).astype(out[name].dtype)
    return out
```

```python
from contextlib import ExitStack

import concourse.bass as bass
from concourse import mybir

STAGES = 5

P = 128
B = 4
D = 192
DC = 2
DK = D // DC
NP_ = 256
JT = NP_ // P
TAIL = B * JT
NT = TAIL + 1
L = NP_ + 1
QUAD = 32
LN_EPS = 1e-5

F32 = mybir.dt.float32
I32 = mybir.dt.int32
BF16 = mybir.dt.bfloat16
ALU = mybir.AluOpType
ACT = mybir.ActivationFunctionType
AXX = mybir.AxisListType.X
ds = bass.ds


def bc(ap, axis, n):
    v = ap.unsqueeze(axis)
    return v.broadcast_to([*v.shape[:axis], n, *v.shape[axis + 1:]])


class Core:

    def __init__(self, nc, ctx):
        self.nc, self.ctx = nc, ctx
        self.in_stage, self.stage_sems = False, []
        self.ps = ctx.enter_context(nc.psum_tensor("banks", [P, 8, 512], F32))
        self.ident = self.sb("ident", [P, P])
        self.h = self.sb("h", [P, NT, D])
        self.xn = self.sb("xn", [P, NT, D])
        self.xt = self.sb("xt", [DK, DC, NT * P])
        self.stats = self.sb("stats", [P, NT, 6])
        self.mv = self.sb("mv", [P, NT, 2])
        self.veps = self.sb("veps", [P, NT])
        self.half = self.sb("half", [P, NT])
        self.rs = self.sb("rs", [P, NT])
        self.ones = self.sb("ones", [P, P])
        self.s_half, self.s_ones = self.sem("half_ready"), self.sem("ones_ready")
        self.preload = []
        self.s_ident = self.sem("ident_loaded")

    def sb(self, name, shape, dt=F32, ctx=None):
        return (ctx or self.ctx).enter_context(self.nc.sbuf_tensor(name, shape, dt))

    def sem(self, name):
        s = self.nc.alloc_semaphore(name=name)
        if self.in_stage:
            self.stage_sems.append(s)
        return s


class Norm:

    def __init__(self, k, tag):
        self.k = k
        self.stats = k.sem(f"{tag}_norm_stats")
        self.moments = k.sem(f"{tag}_norm_moments")
        self.veps = k.sem(f"{tag}_norm_veps")
        self.rstd = k.sem(f"{tag}_norm_rstd")
        self.normed = k.sem(f"{tag}_norm_normed")
        self.turned = k.sem(f"{tag}_norm_turned")
        self.xt_ready = k.sem(f"{tag}_norm_xt_ready")

    def vector(self, dve):
        k = self.k
        for t in range(NT):
            dve.bn_stats(k.stats[:, t, :], k.h[:, t, :]).then_inc(self.stats, 1)
        for t in range(NT):
            dve.wait_ge(self.stats, t + 1)
            dve.bn_aggr(k.mv[:, t, :], k.stats[:, t, :]).then_inc(self.moments, 1)
        dve.wait_ge(self.moments, NT)
        dve.tensor_scalar(k.veps[:, :], k.mv[:, :, 1], LN_EPS, None, ALU.add).then_inc(self.veps, 1)
        dve.wait_ge(self.rstd, 1)
        for t in range(NT):
            dve.tensor_scalar(k.xn[:, t, :], k.h[:, t, :], k.mv[:, t, 0:1], k.rs[:, t:t + 1],
                              ALU.subtract, ALU.mult).then_inc(self.normed, 1)

    def gpsimd(self, pool):
        k = self.k
        pool.wait_ge(self.veps, 1)
        pool.tensor_tensor(k.rs[:, :], k.veps[:, :], k.half[:, :], ALU.pow).then_inc(self.rstd, 1)

    def tensor(self, pe, src_ready=None):
        k = self.k
        src_ready = src_ready or self.normed
        for t in range(NT):
            pe.wait_ge(src_ready, t + 1)
            for c in range(DC):
                at = (t % 2) * 2 * P + c * P
                mm = pe.transpose(k.ps[0:DK, t // 2, at:at + P], k.xn[:, t, c * DK:(c + 1) * DK],
                                  k.ident[:, :])
            mm.then_inc(self.turned, 1)

    def scalar(self, act):
        k = self.k
        for g in range((NT + 1) // 2):
            n = min(2, NT - 2 * g)
            act.wait_ge(self.turned, 2 * g + n)
            act.activation(
                k.xt[:, :, 2 * g * P:(2 * g + n) * P].rearrange("p c (t q) -> p t c q", t=n),
                k.ps[0:DK, g, 0:2 * n * P].rearrange("p (t c q) -> p t c q", t=n, c=DC),
                ACT.Copy).then_inc(self.xt_ready, 1)


NORM_BANKS = (NT + 1) // 2

E_TOK = 64
G_TOK = 16
FEAT = (3, 12, 48)
ROWS = (4096, 1024, 256)


def stage_tok(k, a):
    nc, ps = k.nc, k.ps
    with ExitStack() as st:
        def sb(name, shape, dt=F32):
            return k.sb(name, shape, dt, st)

        idx0 = sb("idx0", [P, 32], I32)
        idx1 = sb("idx1", [P, 8], I32)
        idx2 = sb("idx2", [P, 2], I32)
        g0 = sb("g0", [P, 2, G_TOK, B * 3])
        g1 = sb("g1", [P, 8, B * 12])
        g2 = sb("g2", [P, 2, B * 48])
        g0b = sb("g0b", [P, 2, B, G_TOK * 3])
        g1b = sb("g1b", [P, B, 8 * 12])
        w0 = sb("w0", [48, E_TOK])
        w1 = sb("w1", [96, 2, E_TOK])
        w2 = sb("w2", [48, G_TOK, E_TOK])
        tb = sb("tb", [E_TOK, 3])
        wf = sb("wf", [E_TOK, 3, D])
        up1 = sb("up1", [E_TOK + 1, NP_])
        up2 = sb("up2", [16, NP_])
        x0t = sb("x0t", [48, B * NP_])
        x1t = sb("x1t", [96, B, 2, 64])
        x2t = sb("x2t", [48, 2, B, P])
        y0t = sb("y0t", [E_TOK, B * NP_])
        y1t = sb("y1t", [E_TOK, B * 64])
        y2t = sb("y2t", [E_TOK, B * 16])
        z1 = sb("z1", [E_TOK + 1, B, D])
        z2 = sb("z2", [16, B, D])

        idx_in = k.sem("tok_idx_loaded")
        w_in = k.sem("tok_weights_loaded")
        cls_zero = k.sem("tok_cls_rows_zero")
        cls_in = k.sem("tok_cls_loaded")
        got = [k.sem(f"tok_gathered{i}") for i in range(3)]
        got0 = [got[0], k.sem("tok_gathered0b")]
        by1, by0 = k.sem("tok_by_image1"), k.sem("tok_by_image0")
        tr2, tr1, tr0 = (k.sem(f"tok_turned{i}") for i in (2, 1, 0))
        xt2, xt1, xt0 = (k.sem(f"tok_xt{i}") for i in (2, 1, 0))
        ym2, ym1, ym0 = (k.sem(f"tok_y{i}") for i in (2, 1, 0))
        yr2, yr1, yr0 = (k.sem(f"tok_yt{i}") for i in (2, 1, 0))
        yr0 = [yr0, k.sem("tok_yt0b")]
        zm2, zm1, zr2, zr1 = (k.sem(f"tok_{n}") for n in ("z2", "z1", "z2_copied", "z1_copied"))
        hm, hr = k.sem("tok_h"), k.sem("tok_h_copied")

        with nc.Block() as block:
            @block.sync
            def _(sp):
                sp.dma_start(idx2[:, :], a["idx2"]).then_inc(idx_in, 16)
                sp.dma_start(idx1[:, :], a["idx1"]).then_inc(idx_in, 16)
                sp.dma_start(idx0[:, :], a["idx0"]).then_inc(idx_in, 16)
                sp.dma_start(k.ident[:, :], a["ident"]).then_inc(k.s_ident, 16)
                sp.dma_start(w2[:, :, :], a["tw2"]).then_inc(w_in, 16)
                sp.dma_start(w1[:, :, :], a["tw1"]).then_inc(w_in, 16)
                sp.dma_start(w0[:, :], a["tw0"]).then_inc(w_in, 16)
                sp.dma_start(tb[:, :], a["tb"]).then_inc(w_in, 16)
                sp.dma_start(wf[:, :, :], a["twf"]).then_inc(w_in, 16)
                sp.dma_start(up1[:, :], a["up1"]).then_inc(w_in, 16)
                sp.dma_start(up2[:, :], a["up2"]).then_inc(w_in, 16)
                for b in range(B):
                    sp.dma_start(z1[E_TOK:E_TOK + 1, b, :], a["tbf"]).then_inc(w_in, 16)
                sp.wait_ge(cls_zero, 1)
                for b in range(B):
                    sp.dma_start(k.h[QUAD * b:QUAD * b + 1, TAIL, :], a["cls"]).then_inc(cls_in, 16)
                for dst, src, loaded in k.preload:
                    sp.dma_start(dst, src).then_inc(loaded, 16)
                sp.wait_ge(cls_in, 16 * B)

            @block.gpsimd
            def _(pool):
                pool.memset(k.h[:, TAIL, :], 0.0).then_inc(cls_zero, 1)
                pool.memset(k.half[:, :], -0.5).then_inc(k.s_half, 1)
                pool.memset(k.ones[:, :], 1.0).then_inc(k.s_ones, 1)
                pool.wait_ge(idx_in, 48)
                for j in range(2):
                    pool.indirect_dma_start(g2[:, j, :], None, a["x2"],
                                            bass.IndirectOffsetOnAxis(ap=idx2[:, j:j + 1], axis=0)
                                            ).then_inc(got[2], 16)
                for j in range(8):
                    pool.indirect_dma_start(g1[:, j, :], None, a["x1"],
                                            bass.IndirectOffsetOnAxis(ap=idx1[:, j:j + 1], axis=0)
                                            ).then_inc(got[1], 16)
                for j in range(32):
                    pool.indirect_dma_start(g0[:, j // G_TOK, j % G_TOK, :], None, a["x0"],
                                            bass.IndirectOffsetOnAxis(ap=idx0[:, j:j + 1], axis=0)
                                            ).then_inc(got0[j // G_TOK], 16)

            @block.tensor
            def _(pe):
                pe.wait_ge(k.s_ident, 16)
                pe.wait_ge(got[2], 32)
                for j in range(2):
                    for b in range(B):
                        mm = pe.transpose(ps[0:48, j, b * P:(b + 1) * P],
                                          g2[:, j, b * 48:(b + 1) * 48], k.ident[:, :])
                    mm.then_inc(tr2, 1)
                pe.wait_ge(w_in, 16 * (7 + B))
                pe.wait_ge(xt2, 2)
                for g in range(G_TOK):
                    mm = pe.matmul(ps[0:E_TOK, 2, 0:64].rearrange("p (b t) -> p b t", b=B),
                                   w2[:, g, :], x2t[:, g // 8, :, (g % 8) * 16:(g % 8 + 1) * 16],
                                   start=g == 0, stop=g == G_TOK - 1)
                mm.then_inc(ym2, 1)
                pe.wait_ge(yr2, 1)
                for b in range(B):
                    mm = pe.matmul(ps[0:16, 3 + b // 2, (b % 2) * D:(b % 2 + 1) * D],
                                   y2t[:, b * 16:(b + 1) * 16], wf[:, 2, :], start=True, stop=True)
                mm.then_inc(zm2, 1)
                pe.wait_ge(by1, 1)
                for b in range(B):
                    mm = pe.transpose(ps[0:96, 5, b * P:(b + 1) * P],
                                      g1b[:, b, :], k.ident[:, :])
                mm.then_inc(tr1, 1)
                pe.wait_ge(xt1, 1)
                for c in range(2):
                    mm = pe.matmul(ps[0:E_TOK, 2, 256:512].rearrange("p (b t) -> p b t", b=B),
                                   w1[:, c, :], x1t[:, :, c, :], start=c == 0, stop=c == 1)
                mm.then_inc(ym1, 1)
                pe.wait_ge(yr1, 1)
                for b in range(B):
                    mm = pe.matmul(ps[0:64, 6 + b // 2, (b % 2) * D:(b % 2 + 1) * D],
                                   y1t[:, b * 64:(b + 1) * 64], wf[:, 1, :], start=True, stop=True)
                mm.then_inc(zm1, 1)
                for i in range(2):
                    pe.wait_ge(by0, i + 1)
                    for b in range(B):
                        mm = pe.transpose(ps[0:48, i, b * P:(b + 1) * P],
                                          g0b[:, i, b, :], k.ident[:, :])
                    mm.then_inc(tr0, 1)
                pe.wait_ge(xt0, 2)
                for i in range(2):
                    pe.matmul(ps[0:E_TOK, 2 if i == 0 else 5, :], w0[:, :],
                              x0t[:, i * 512:(i + 1) * 512], start=True, stop=True).then_inc(ym0, 1)
                pe.wait_ge(zr2, 2)
                pe.wait_ge(zr1, 2)
                for t in range(TAIL):
                    b, j = t // JT, t % JT
                    out = ps[:, (3, 4, 6, 7)[b], j * D:(j + 1) * D]
                    pe.wait_ge(yr0[b // 2], 1)
                    pe.matmul(out, y0t[:, t * P:(t + 1) * P], wf[:, 0, :], start=True, stop=False)
                    pe.matmul(out, up1[:, j * P:(j + 1) * P], z1[:, b, :], start=False, stop=False)
                    pe.matmul(out, up2[:, j * P:(j + 1) * P], z2[:, b, :], start=False,
                              stop=True).then_inc(hm, 1)

            @block.scalar
            def _(act):
                for i in range(2):
                    act.wait_ge(tr2, i + 1)
                    act.activation(x2t[:, i, :, :].rearrange("p b q -> p (b q)"), ps[0:48, i, :],
                                   ACT.Copy).then_inc(xt2, 1)
                act.wait_ge(zm2, 1)
                for i in range(2):
                    act.activation(z2[:, 2 * i:2 * i + 2, :].rearrange("p b d -> p (b d)"),
                                   ps[0:16, 3 + i, 0:2 * D], ACT.Copy).then_inc(zr2, 1)
                act.wait_ge(zm1, 1)
                for i in range(2):
                    act.activation(z1[0:64, 2 * i:2 * i + 2, :].rearrange("p b d -> p (b d)"),
                                   ps[0:64, 6 + i, 0:2 * D], ACT.Copy).then_inc(zr1, 1)
                act.wait_ge(ym0, 2)
                act.activation(y0t[:, 512:1024], ps[0:E_TOK, 5, :], ACT.Identity,
                               bias=tb[:, 0:1]).then_inc(yr0[1], 1)

            @block.vector
            def _(dve):
                dve.wait_ge(ym2, 1)
                dve.tensor_scalar(y2t[:, :], ps[0:E_TOK, 2, 0:64], tb[:, 2:3], None,
                                  ALU.add).then_inc(yr2, 1)
                dve.wait_ge(got[1], 128)
                dve.tensor_copy(g1b[:, :, :].rearrange("p b (j f) -> p b j f", j=8),
                                g1[:, :, :].rearrange("p j (b f) -> p b j f", b=B)).then_inc(by1, 1)
                dve.wait_ge(tr1, 1)
                dve.tensor_copy(x1t[:, :, :, :].rearrange("p b a t -> p (b a t)"),
                                ps[0:96, 5, :]).then_inc(xt1, 1)
                dve.wait_ge(ym1, 1)
                dve.tensor_scalar(y1t[:, :], ps[0:E_TOK, 2, 256:512], tb[:, 1:2], None,
                                  ALU.add).then_inc(yr1, 1)
                for i in range(2):
                    dve.wait_ge(got0[i], 256)
                    dve.tensor_copy(g0b[:, i, :, :].rearrange("p b (g c) -> p b g c", c=3),
                                    g0[:, i, :, :].rearrange("p g (b c) -> p b g c", b=B)
                                    ).then_inc(by0, 1)
                for i in range(2):
                    dve.wait_ge(tr0, i + 1)
                    dve.tensor_copy(
                        x0t[:, :].rearrange("p (b j q) -> p b j q", b=B, j=2)[:, :, i, :],
                        ps[0:48, i, :].rearrange("p (b q) -> p b q", b=B)).then_inc(xt0, 1)
                dve.wait_ge(ym0, 1)
                dve.tensor_scalar(y0t[:, 0:512], ps[0:E_TOK, 2, :], tb[:, 0:1], None,
                                  ALU.add).then_inc(yr0[0], 1)
                for b in range(B):
                    dve.wait_ge(hm, JT * (b + 1))
                    dve.tensor_copy(k.h[:, JT * b:JT * b + JT, :].rearrange("p t d -> p (t d)"),
                                    ps[:, (3, 4, 6, 7)[b], 0:JT * D]).then_inc(hr, 1)


def store(k, out):
    stored = k.sem("out_stored")
    with k.nc.Block() as block:
        @block.sync
        def _(sp):
            for b in range(B):
                sp.dma_start(out[b, 1:L, :].rearrange("(j p) d -> p j d", p=P),
                             k.h[:, JT * b:JT * (b + 1), :]).then_inc(stored, 16)
                sp.dma_start(out[b, 0:1, :], k.h[QUAD * b:QUAD * b + 1, TAIL, :]).then_inc(stored, 16)
            sp.wait_ge(stored, 16 * 2 * B)


HEADS = 12
DH = D // HEADS
HC = 3
SC = 196
NK = L + SC
KT = 4
KR = -(-NK // KT)
NKP = KT * KR
STEPS = HEADS * JT + 1


def alloc_attn(k, a, st):
    k.wq = k.sb("wq", [DK, DC, HC * P], F32, st)
    k.wk = k.sb("wk", [DK, DC, HC * P], F32, st)
    k.wv = k.sb("wv", [DK, DC, D], F32, st)
    k.wp = k.sb("wp", [DK, DC, D], F32, st)
    k.bp = k.sb("bp", [1, D], F32, st)
    k.head_of_row = k.sb("head_of_row", [P, HC, HEADS], F32, st)
    k.head_dims = k.sb("head_dims", [HEADS, D], F32, st)
    k.xb = k.sb("xb", [DK, DC, NKP], F32, st)
    k.s_attn_w = k.sem("attn_weights_loaded")
    k.preload += [(dst, a[n], k.s_attn_w) for dst, n in (
        (k.wq[:, :, :], "wq"), (k.wk[:, :, :], "wk"), (k.wv[:, :, :], "wv"), (k.wp[:, :, :], "wp"),
        (k.bp[:, :], "bp"), (k.head_of_row[:, :, :], "head_of_row"),
        (k.head_dims[:, :], "head_dims"), (k.xb[:, :, L:NKP], "sct"))]


def stage_attn(k, a):
    nc, ps = k.nc, k.ps
    with ExitStack() as st:
        def sb(name, shape, dt=F32):
            return k.sb(name, shape, dt, st)

        qt = sb("qt", [P, HC, L])
        kt = sb("kt", [P, HC, NKP])
        vt = sb("vt", [KR, KT, D])
        qc = sb("qc", [P, HC, HEADS])
        prob = sb("prob", [P, 3, NKP])
        pt = sb("pt", [KR, 3, KT * P])
        nmax = sb("nmax", [P, STEPS])
        rsum = sb("rsum", [P, STEPS])
        rinv = sb("rinv", [P, STEPS])
        on = sb("on", [P, JT, D])
        oc = sb("oc", [HEADS, D])
        ot = sb("ot", [DK, JT, DC, P])
        otc = sb("otc", [DK, DC, P])

        norm = Norm(k, "attn")
        xb_r = k.sem("attn_xb_ready")
        zero = k.sem("attn_pads_zero")
        q_m, k_m, v_m = (k.sem(f"attn_{n}_product") for n in "qkv")
        q_r, k_r, v_r = (k.sem(f"attn_{n}_ready") for n in "qkv")
        qc_r = k.sem("attn_cls_q_ready")
        score, negmax, exped = (k.sem(f"attn_{n}") for n in ("scores", "negmax", "exp"))
        turned, pt_r, pv = (k.sem(f"attn_{n}") for n in ("probs_turned", "pt_ready", "pv"))
        rinv_r, on_r, on_t, ot_r = (k.sem(f"attn_{n}") for n in ("rinv", "out_scaled", "out_turned", "ot"))
        otc_m, otc_r, proj, h_r = (k.sem(f"attn_{n}") for n in ("cls_turned", "cls_ot", "proj", "h_added"))
        proj_c = k.sem("attn_cls_proj")
        LAG = 2

        with nc.Block() as block:
            @block.gpsimd
            def _(pool):
                pool.memset(prob[:, :, NK:NKP], 0.0).then_inc(zero, 1)
                pool.memset(otc[:, :, :], 0.0).then_inc(zero, 1)
                norm.gpsimd(pool)

            @block.tensor
            def _(pe):
                norm.tensor(pe)
                pe.wait_ge(k.s_attn_w, 16 * 8)
                pe.wait_ge(k.s_ones, 1)
                pe.wait_ge(zero, 2)
                pe.wait_ge(norm.xt_ready, NORM_BANKS)
                with pe.Fori(0, B) as i:
                    pe.wait_ge(xb_r, i * 2 + 2)
                    for c in range(HC):
                        for d in range(DC):
                            mm = pe.matmul(ps[:, c, 0:L], k.wq[:, d, c * P:(c + 1) * P],
                                           k.xb[:, d, 0:L], start=d == 0, stop=d == DC - 1)
                        mm.then_inc(q_m, 1)
                    for c in range(HC):
                        for d in range(DC):
                            mm = pe.matmul(ps[:, 3 + c, 0:NKP], k.wk[:, d, c * P:(c + 1) * P],
                                           k.xb[:, d, :], start=d == 0, stop=d == DC - 1)
                        mm.then_inc(k_m, 1)
                    for t in range(KT):
                        for d in range(DC):
                            mm = pe.matmul(ps[0:KR, 6 + t // 2, (t % 2) * D:(t % 2 + 1) * D],
                                           k.xb[:, d, t * KR:(t + 1) * KR], k.wv[:, d, :],
                                           start=d == 0, stop=d == DC - 1)
                        mm.then_inc(v_m, 1)

                    def scores(s):
                        h, j = s // JT, s % JT
                        c, g = h // 4, h % 4
                        if s < 3:
                            pe.wait_ge(q_r, i * HC + HC)
                            pe.wait_ge(k_r, i * HC + HC)
                        else:
                            pe.wait_ge(exped, i * STEPS + s - 2)
                        if s < STEPS - 1:
                            row = slice(QUAD * g, QUAD * g + DH)
                            pe.matmul(ps[:, s % 3, 0:NK], qt[row, c, j * P:(j + 1) * P],
                                      kt[row, c, 0:NK], start=True, stop=True).then_inc(score, 1)
                        else:
                            pe.wait_ge(qc_r, i + 1)
                            for c in range(HC):
                                mm = pe.matmul(ps[0:HEADS, s % 3, 0:NK], qc[:, c, :], kt[:, c, 0:NK],
                                               start=c == 0, stop=c == HC - 1)
                            mm.then_inc(score, 1)

                    def turn(s):
                        pe.wait_ge(exped, i * STEPS + s + 1)
                        if s >= 3:
                            pe.wait_ge(pt_r, i * STEPS + s - 2)
                        for t in range(KT):
                            mm = pe.transpose(ps[0:KR, 3 + s % 3, t * P:(t + 1) * P],
                                              prob[:, s % 3, t * KR:(t + 1) * KR], k.ident[:, :])
                        mm.then_inc(turned, 1)

                    def values(s):
                        pe.wait_ge(pt_r, i * STEPS + s + 1)
                        if s == 0:
                            pe.wait_ge(v_r, i * 2 + 2)
                        h, j = s // JT, s % JT
                        for t in range(KT):
                            if s < STEPS - 1:
                                mm = pe.matmul(ps[:, 6 + j, h * DH:(h + 1) * DH],
                                               pt[:, s % 3, t * P:(t + 1) * P],
                                               vt[:, t, h * DH:(h + 1) * DH],
                                               start=t == 0, stop=t == KT - 1)
                            else:
                                mm = pe.matmul(ps[0:HEADS, 6, 256:256 + D],
                                               pt[:, s % 3, t * P:t * P + HEADS], vt[:, t, :],
                                               start=t == 0, stop=t == KT - 1)
                        mm.then_inc(pv, 1)

                    for s in range(STEPS + LAG + 1):
                        if s < STEPS:
                            scores(s)
                        if 0 <= s - LAG < STEPS:
                            turn(s - LAG)
                        if s - LAG - 1 >= 0:
                            values(s - LAG - 1)
                    pe.wait_ge(on_r, i * 3 + 3)
                    for d in range(DC):
                        mm = pe.matmul(ps[0:DK, 4, d:d + 1], oc[:, d * DK:(d + 1) * DK],
                                       k.ones[0:HEADS, 0:1], start=True, stop=True)
                    mm.then_inc(otc_m, 1)
                    for j in range(JT):
                        for d in range(DC):
                            at = (j * DC + d) * P
                            mm = pe.transpose(ps[0:DK, 3, at:at + P], on[:, j, d * DK:(d + 1) * DK],
                                              k.ident[:, :])
                    mm.then_inc(on_t, 1)
                    pe.wait_ge(ot_r, i + 1)
                    for j in range(JT):
                        out = ps[:, 5, j * D:(j + 1) * D]
                        for d in range(DC):
                            pe.matmul(out, ot[:, j, d, :], k.wp[:, d, :], start=d == 0, stop=False)
                        mm = pe.matmul(out, k.ones[0:1, :], k.bp[:, :], start=False, stop=True)
                    mm.then_inc(proj, 1)
                pe.wait_ge(otc_r, B)
                out = ps[:, 4, 0:D]
                for d in range(DC):
                    pe.matmul(out, otc[:, d, :], k.wp[:, d, :], start=d == 0, stop=False)
                pe.matmul(out, k.ones[0:1, :], k.bp[:, :], start=False, stop=True).then_inc(proj_c, 1)

            @block.scalar
            def _(act):
                norm.scalar(act)
                with act.Fori(0, B) as i:
                    for c in range(HC):
                        act.wait_ge(q_m, i * HC + c + 1)
                        act.activation(qt[:, c, :], ps[:, c, 0:L], ACT.Copy,
                                       scale=DH ** -0.5).then_inc(q_r, 1)
                    for t in range(2):
                        act.wait_ge(v_m, i * KT + 2 * t + 2)
                        act.activation(vt[:, 2 * t:2 * t + 2, :].rearrange("p t d -> p (t d)"),
                                       ps[0:KR, 6 + t, 0:2 * D], ACT.Copy).then_inc(v_r, 1)
                    for s in range(STEPS):
                        n = P if s < STEPS - 1 else HEADS
                        act.wait_ge(negmax, i * STEPS + s + 1)
                        if s >= 3:
                            act.wait_ge(turned, i * STEPS + s - 2)
                        act.activation(prob[0:n, s % 3, 0:NK], ps[0:n, s % 3, 0:NK], ACT.Exp,
                                       bias=nmax[0:n, s:s + 1],
                                       accum_out=rsum[0:n, s:s + 1]).then_inc(exped, 1)
                    act.wait_ge(on_t, i + 1)
                    act.activation(ot[:, :, :, :].rearrange("p j c q -> p (j c q)"), ps[0:DK, 3, :],
                                   ACT.Copy).then_inc(ot_r, 1)

            @block.vector
            def _(dve):
                norm.vector(dve)
                dve.wait_ge(norm.xt_ready, NORM_BANKS)
                dve.wait_ge(k.s_attn_w, 16 * 8)
                dve.wait_ge(zero, 2)
                with dve.Fori(0, B) as i:
                    dve.tensor_copy(k.xb[:, :, 0:NP_], k.xt[:, :, ds(i * NP_, NP_)]).then_inc(xb_r, 1)
                    dve.tensor_copy(k.xb[:, :, NP_:L],
                                    k.xt[:, :, ds(i * QUAD + TAIL * P, 1)]).then_inc(xb_r, 1)
                    for c in range(HC):
                        dve.wait_ge(k_m, i * HC + c + 1)
                        dve.tensor_copy(kt[:, c, :], ps[:, 3 + c, 0:NKP]).then_inc(k_r, 1)
                    dve.wait_ge(q_r, i * HC + HC)
                    dve.tensor_tensor(qc[:, :, :], qt[:, :, NP_:L].broadcast_to([P, HC, HEADS]),
                                      k.head_of_row[:, :, :], ALU.mult).then_inc(qc_r, 1)

                    def copy(s):
                        n = P if s < STEPS - 1 else HEADS
                        dve.wait_ge(turned, i * STEPS + s + 1)
                        if s >= 3:
                            dve.wait_ge(pv, i * STEPS + s - 2)
                        dve.tensor_copy(
                            pt[:, s % 3, :].rearrange("p (t q) -> p t q", t=KT)[:, :, 0:n],
                            ps[0:KR, 3 + s % 3, :].rearrange("p (t q) -> p t q", t=KT)[:, :, 0:n]
                        ).then_inc(pt_r, 1)

                    for s in range(STEPS + LAG):
                        if s < STEPS:
                            n = P if s < STEPS - 1 else HEADS
                            dve.wait_ge(score, i * STEPS + s + 1)
                            dve.tensor_reduce(nmax[0:n, s:s + 1], ps[0:n, s % 3, 0:NK], AXX, ALU.max,
                                              negate=True).then_inc(negmax, 1)
                        if s >= LAG:
                            copy(s - LAG)
                    dve.wait_ge(exped, i * STEPS + STEPS)
                    dve.reciprocal(rinv[:, 0:STEPS - 1], rsum[:, 0:STEPS - 1]).then_inc(rinv_r, 1)
                    dve.reciprocal(rinv[0:HEADS, STEPS - 1:STEPS],
                                   rsum[0:HEADS, STEPS - 1:STEPS]).then_inc(rinv_r, 1)
                    dve.wait_ge(rinv_r, i * 2 + 2)
                    dve.wait_ge(pv, i * STEPS + STEPS)
                    for j in range(JT):
                        dve.tensor_tensor(
                            on[:, j, :].rearrange("p (h d) -> p h d", h=HEADS),
                            ps[:, 6 + j, 0:D].rearrange("p (h d) -> p h d", h=HEADS),
                            bc(rinv[:, j:STEPS - 1:JT], 2, DH), ALU.mult).then_inc(on_r, 1)
                    dve.scalar_tensor_tensor(oc[:, :], ps[0:HEADS, 6, 256:256 + D],
                                             rinv[0:HEADS, STEPS - 1:STEPS], k.head_dims[:, :],
                                             ALU.mult, ALU.mult).then_inc(on_r, 1)
                    dve.wait_ge(otc_m, i + 1)
                    dve.tensor_copy(otc[:, :, ds(i * QUAD, 1)],
                                    ps[0:DK, 4, 0:DC].unsqueeze(2)).then_inc(otc_r, 1)
                    dve.wait_ge(proj, i + 1)
                    dve.tensor_tensor(k.h[:, ds(i * JT, JT), :], k.h[:, ds(i * JT, JT), :],
                                      ps[:, 5, 0:JT * D].rearrange("p (j d) -> p j d", j=JT),
                                      ALU.add).then_inc(h_r, 1)
                dve.wait_ge(proj_c, 1)
                dve.tensor_tensor(k.h[:, TAIL, :], k.h[:, TAIL, :], ps[:, 4, 0:D],
                                  ALU.add).then_inc(h_r, 1)


def layout_attn(i):
    import numpy as np

    def rows(w):
        return w.reshape(DC, DK, -1).transpose(1, 0, 2)

    def quarters(w):
        o = np.zeros((D, HEADS, QUAD), w.dtype)
        o[:, :, :DH] = w.reshape(D, HEADS, DH)
        return rows(o.reshape(D, HC * P))

    w = i["L0_attn_W_qkv"]
    sct = np.zeros((D, NKP - L), np.float32)
    sct[:, :SC] = i["L0_attn_sc_token"][0].T
    head = np.zeros((P, HC, HEADS), np.float32)
    for h in range(HEADS):
        head[QUAD * (h % 4):QUAD * (h % 4) + DH, h // 4, h] = 1
    return {
        "wq": quarters(w[:, 0:D]), "wk": quarters(w[:, D:2 * D]), "wv": rows(w[:, 2 * D:]),
        "wp": rows(i["L0_attn_W_proj"]), "bp": i["L0_attn_b_proj"].reshape(1, D), "sct": rows(sct),
        "head_of_row": head, "head_dims": np.repeat(np.eye(HEADS, dtype=np.float32), DH, axis=1),
    }


EX = 32
SL = 32
ES = EX * SL
HID = 768
HJ = HID // P
R = P // SL
EC = EX // R
L2_TINY = 1e-24


def alloc_soft(k, a, st):
    k.w1 = [k.sb(f"soft_w1_{r}", [DK, DC, HID], F32, st) for r in range(R)]
    k.w2 = [k.sb(f"soft_w2_{r}", [P, HJ, D], F32, st) for r in range(R)]
    k.b1 = k.sb("soft_b1", [P, EX, HJ], F32, st)
    k.b2 = k.sb("soft_b2", [EX, D], F32, st)
    k.scale = k.sb("soft_scale", [DK, 1], F32, st)
    k.s_w = [k.sem(f"soft_w_loaded{r}") for r in range(R)]
    k.s_soft = k.sem("soft_small_loaded")
    k.preload += [(k.b1[:, :, :], a["sb1"], k.s_soft), (k.b2[:, :], a["sb2"], k.s_soft),
                  (k.scale[:, :], a["sscale"].broadcast_to([DK, 1]), k.s_soft)]
    for r in range(R):
        k.preload += [(k.w1[r][:, :, :], a["sw1"][r], k.s_w[r]), (k.w2[r][:, :, :], a["sw2"][r], k.s_w[r])]


def stage_soft(k, a):
    nc, ps = k.nc, k.ps
    with ExitStack() as st:
        slots = k.sb("slots", [DK, DC, EX, B * SL], F32, st)
        cwt = k.sb("combine_t", [P, EC, NT * P], F32, st)
        cst = k.sb("expert_share_t", [EX, NT * P], F32, st)
        soft_dispatch(k, a, slots, cwt, cst)
        soft_experts(k, a, slots, cwt, cst)


def soft_dispatch(k, a, slots, cwt, cst):
    nc, ps = k.nc, k.ps
    ORDER = [TAIL, *range(TAIL)]
    with ExitStack() as st:
        def sb(name, shape, dt=F32):
            return k.sb(name, shape, dt, st)

        phi = sb("phi", [DK, DC, ES])
        ex = sb("ex", [P, 2, ES])
        dw = sb("dw", [P, 3, ES])
        dwc = sb("dwc", [P, ES])
        cw = sb("cw", [P, 2, ES])
        half = sb("half_wide", [DK, ES])
        ss = sb("ss", [P, NT])
        ssm = sb("ssm", [P, NT])
        rn = sb("rn", [P, NT])
        me = sb("me", [P, NT, EX])
        ngm = sb("ngm", [P, NT])
        f0 = sb("f0", [P, NT, EX])
        se = sb("se", [P, NT, EX])
        fs = sb("fs", [P, NT, EX])
        z = sb("z", [P, NT])
        zi = sb("zi", [P, NT])
        g = sb("g", [P, NT, EX])
        f = sb("f", [P, NT, EX])
        cs = sb("cs", [P, NT, EX])
        sq = ex
        pn = cw[0:DK, 0, :]
        pr = cw[0:DK, 1, :]

        norm = Norm(k, "soft")
        phi_in = k.sem("soft_phi_loaded")
        half_r, sq_r, colsum, pn_r, pr_r, ph1, phin = (
            k.sem(f"soft_{n}") for n in ("half", "squares", "colsum", "phi_norms", "phi_rnorms",
                                         "phi_unit", "phi_ready"))
        ss_r, ssm_r, rn_r, xl_r = (k.sem(f"soft_{n}") for n in ("ss", "ssm", "rn", "unit"))
        logit, me_r, ngm_r, sub, exped, f0_r = (
            k.sem(f"soft_{n}") for n in ("logits", "expert_max", "max", "shifted", "exp", "max_factor"))
        se_r, fs_r, zi_r, f_r, cs_r, dw_r, cw_r, g_r = (
            k.sem(f"soft_{n}") for n in ("sums", "weighted_sums", "zinv", "f", "share", "dw", "cw", "g"))
        cw_t, cwt_r, sl_m, sl_r, cs_t, cst_r = (
            k.sem(f"soft_{n}") for n in ("cw_turned", "cwt_ready", "slots_product", "slots_ready",
                                         "share_turned", "share_ready"))

        with nc.Block() as block:
            @block.sync
            def _(sp):
                sp.dma_start(phi[:, :, :], a["phi"]).then_inc(phi_in, 16)

            @block.gpsimd
            def _(pool):
                pool.memset(half[:, :], -0.5).then_inc(half_r, 1)
                norm.gpsimd(pool)
                pool.wait_ge(half_r, 1)
                pool.wait_ge(pn_r, 1)
                pool.tensor_tensor(pr, pn, half[:, :], ALU.pow).then_inc(pr_r, 1)
                pool.wait_ge(ssm_r, 1)
                pool.tensor_tensor(rn[:, :], ssm[:, :], k.half[:, :], ALU.pow).then_inc(rn_r, 1)
                for n, t in enumerate(ORDER):
                    pool.wait_ge(f_r, n + 1)
                    if n == 0:
                        pool.wait_ge(phin, DC)
                    if n >= 2:
                        pool.wait_ge(cw_t, n - 1)
                    pool.tensor_tensor(cw[:, n % 2, :].rearrange("p (e s) -> p e s", e=EX),
                                       ex[:, n % 2, :].rearrange("p (e s) -> p e s", e=EX),
                                       bc(f[:, t, :], 2, SL), ALU.mult).then_inc(cw_r, 1)

            @block.tensor
            def _(pe):
                pe.wait_ge(sq_r, 2)
                for c in range(2):
                    for d in range(DC):
                        mm = pe.matmul(ps[0:DK, 5 + c, :], k.ones[0:DK, 0:DK],
                                       sq[0:DK, d, c * 512:(c + 1) * 512], start=d == 0, stop=d == DC - 1)
                mm.then_inc(colsum, 1)
                norm.tensor(pe, xl_r)
                pe.wait_ge(phin, DC)
                pe.wait_ge(norm.xt_ready, NORM_BANKS)

                def logits(n):
                    t = ORDER[n]
                    if n >= 2:
                        pe.wait_ge(sub, n - 1)
                    for c in range(2):
                        for d in range(DC):
                            mm = pe.matmul(ps[:, 2 * (n % 2) + c, :], k.xt[:, d, t * P:(t + 1) * P],
                                           phi[:, d, c * 512:(c + 1) * 512], start=d == 0, stop=d == DC - 1)
                    mm.then_inc(logit, 1)

                def turn(n):
                    pe.wait_ge(cw_r, n + 1)
                    if n >= 1:
                        pe.wait_ge(cwt_r, 2 * n)
                    for e in range(EC):
                        mm = pe.transpose(ps[:, 4 + e // 4, (e % 4) * P:(e % 4 + 1) * P],
                                          cw[:, n % 2, e * P:(e + 1) * P], k.ident[:, :])
                    mm.then_inc(cw_t, 1)

                def slot_inputs(b):
                    pe.wait_ge(dw_r, 2 * b + 3)
                    for q in range(4):
                        d, c = q // 2, q % 2
                        m = 4 * b + q
                        if m >= 2:
                            pe.wait_ge(sl_r, m - 1)
                        out = ps[0:DK, 6 + m % 2, :]
                        dim, col = slice(d * DK, (d + 1) * DK), slice(c * 512, (c + 1) * 512)
                        for j in range(JT):
                            pe.matmul(out, k.xn[:, 2 * b + j, dim], dw[:, (2 * b + j) % 3, col],
                                      start=j == 0, stop=False)
                        row = slice(QUAD * b, QUAD * b + 1)
                        pe.matmul(out, k.xn[row, TAIL, dim], dwc[row, col], start=False,
                                  stop=True).then_inc(sl_m, 1)

                logits(0)
                logits(1)
                for n in range(NT):
                    turn(n)
                    if n + 2 < NT:
                        logits(n + 2)
                    if n >= 2 and n % 2 == 0:
                        slot_inputs(n // 2 - 1)
                pe.wait_ge(cs_r, NT)
                for t in range(NT):
                    mm = pe.transpose(ps[0:EX, t // 4, (t % 4) * P:(t % 4 + 1) * P], cs[:, t, :],
                                      k.ident[:, :])
                mm.then_inc(cs_t, 1)

            @block.scalar
            def _(act):
                act.wait_ge(phi_in, 16)
                for d in range(DC):
                    act.activation(sq[0:DK, d, :], phi[:, d, :], ACT.Square).then_inc(sq_r, 1)
                for t in range(NT):
                    act.wait_ge(norm.normed, t + 1)
                    act.activation(dw[:, 0, 0:D], k.xn[:, t, :], ACT.Square,
                                   accum_out=ss[:, t:t + 1]).then_inc(ss_r, 1)
                    act.wait_ge(ss_r, t + 1)
                norm.scalar(act)
                for n in range(NT):
                    t = ORDER[n]
                    act.wait_ge(sub, n + 1)
                    act.activation(ex[:, n % 2, :], ex[:, n % 2, :], ACT.Exp).then_inc(exped, 1)
                    act.wait_ge(ngm_r, n + 1)
                    act.activation(f0[:, t, :], me[:, t, :], ACT.Exp,
                                   bias=ngm[:, t:t + 1]).then_inc(f0_r, 1)
                    act.wait_ge(cw_t, n + 1)
                    for c in range(2):
                        act.activation(cwt[:, 4 * c:4 * c + 4, t * P:(t + 1) * P],
                                       ps[:, 4 + c, :].rearrange("p (e q) -> p e q", e=4),
                                       ACT.Copy).then_inc(cwt_r, 1)
                    if n >= 2 and n % 2 == 0:
                        b = n // 2 - 1
                        for q in range(4):
                            d, c = q // 2, q % 2
                            act.wait_ge(sl_m, 4 * b + q + 1)
                            act.activation(slots[:, d, c * 16:(c + 1) * 16, b * SL:(b + 1) * SL],
                                           ps[0:DK, 6 + (4 * b + q) % 2, :].rearrange(
                                               "p (e s) -> p e s", e=16), ACT.Copy).then_inc(sl_r, 1)
                act.wait_ge(cs_t, 1)
                for c in range(3):
                    w = min(512, NT * P - c * 512)
                    act.activation(cst[:, c * 512:c * 512 + w], ps[0:EX, c, 0:w],
                                   ACT.Copy).then_inc(cst_r, 1)

            @block.vector
            def _(dve):
                dve.wait_ge(colsum, 1)
                dve.tensor_scalar(pn, ps[0:DK, 5:7, :].rearrange("p c n -> p (c n)"), L2_TINY, None,
                                  ALU.max).then_inc(pn_r, 1)
                dve.wait_ge(phi_in, 16)
                dve.wait_ge(k.s_soft, 48)
                norm.vector(dve)
                dve.wait_ge(ss_r, NT)
                dve.tensor_scalar(ssm[:, :], ss[:, :], L2_TINY, None, ALU.max).then_inc(ssm_r, 1)
                dve.wait_ge(pr_r, 1)
                for d in range(DC):
                    dve.scalar_tensor_tensor(phi[:, d, :], phi[:, d, :], k.scale[:, 0:1], pr,
                                             ALU.mult, ALU.mult).then_inc(phin, 1)
                dve.wait_ge(rn_r, 1)
                for t in range(NT):
                    dve.tensor_scalar(k.xn[:, t, :], k.xn[:, t, :], rn[:, t:t + 1], None,
                                      ALU.mult).then_inc(xl_r, 1)

                def shift(n):
                    t = ORDER[n]
                    dve.wait_ge(logit, n + 1)
                    x = ps[:, 2 * (n % 2):2 * (n % 2) + 2, :].rearrange("p c (e s) -> p (c e) s", s=SL)
                    dve.tensor_reduce(me[:, t, :], x, AXX, ALU.max).then_inc(me_r, 1)
                    dve.wait_ge(me_r, n + 1)
                    if n >= 2:
                        dve.wait_ge(cw_r, n - 1)
                    else:
                        dve.wait_ge(colsum, 1)
                    dve.tensor_tensor(ex[:, n % 2, :].rearrange("p (e s) -> p e s", e=EX), x,
                                      bc(me[:, t, :], 2, SL), ALU.subtract).then_inc(sub, 1)
                    dve.tensor_reduce(ngm[:, t:t + 1], me[:, t, :], AXX, ALU.max,
                                      negate=True).then_inc(ngm_r, 1)

                shift(0)
                for n in range(NT):
                    t = ORDER[n]
                    if n + 1 < NT:
                        shift(n + 1)
                    dve.wait_ge(exped, n + 1)
                    e3 = ex[:, n % 2, :].rearrange("p (e s) -> p e s", e=EX)
                    dve.tensor_reduce(se[:, t, :], e3, AXX, ALU.add).then_inc(se_r, 1)
                    dve.wait_ge(se_r, n + 1)
                    dve.wait_ge(f0_r, n + 1)
                    dve.scalar_tensor_tensor(fs[:, t, :], f0[:, t, :], 1.0, se[:, t, :], ALU.mult,
                                             ALU.mult, accum_out=z[:, t:t + 1]).then_inc(fs_r, 1)
                    dve.reciprocal(g[:, t, :], se[:, t, :]).then_inc(g_r, 1)
                    dve.wait_ge(fs_r, n + 1)
                    dve.reciprocal(zi[:, t:t + 1], z[:, t:t + 1]).then_inc(zi_r, 1)
                    dve.wait_ge(zi_r, n + 1)
                    dve.tensor_scalar(f[:, t, :], f0[:, t, :], zi[:, t:t + 1], None,
                                      ALU.mult).then_inc(f_r, 1)
                    dve.tensor_scalar(cs[:, t, :], fs[:, t, :], zi[:, t:t + 1], None,
                                      ALU.mult).then_inc(cs_r, 1)
                    dve.wait_ge(g_r, n + 1)
                    if n >= 4:
                        dve.wait_ge(sl_m, 4 * ((t - 3) // 2) + 4)
                    dst = dwc[:, :] if t == TAIL else dw[:, t % 3, :]
                    dve.tensor_tensor(dst.rearrange("p (e s) -> p e s", e=EX), e3,
                                      bc(g[:, t, :], 2, SL), ALU.mult).then_inc(dw_r, 1)


def soft_experts(k, a, slots, cwt, cst):
    nc, ps = k.nc, k.ps
    with ExitStack() as st:
        hid = k.sb("hid", [P, 2, HJ, P], F32, st)
        eo = k.sb("eo", [P, B, EC, D], F32, st)
        l1, gelu, l2, eo_r, used, comb, comb_c, added = (
            k.sem(f"soft_{n}") for n in ("layer1", "gelu", "layer2", "eo_ready", "weights_used",
                                         "combined", "combined_cls", "h_added"))
        FREE = R * B

        with nc.Block() as block:
            @block.sync
            def _(sp):
                with sp.Fori(1, EC) as i:
                    for r in range(R):
                        sp.wait_ge(l2, (i - 1) * R + r + 1)
                        sp.dma_start(k.w1[r][:, :, :], a["sw1"][ds(i * R + r, 1)]).then_inc(k.s_w[r], 16)
                        sp.dma_start(k.w2[r][:, :, :], a["sw2"][ds(i * R + r, 1)]).then_inc(k.s_w[r], 16)

            @block.tensor
            def _(pe):
                def layer1(i, r):
                    pe.wait_ge(k.s_w[r], i * 32 + 32)
                    for j in range(HJ):
                        for d in range(DC):
                            rhs = slots[:, d, ds(i * R + r, 1), :].rearrange("p e n -> p (e n)")
                            mm = pe.matmul(ps[:, 2 * (r % 2) + j // 3, (j % 3) * P:(j % 3 + 1) * P],
                                           k.w1[r][:, d, j * P:(j + 1) * P], rhs,
                                           start=d == 0, stop=d == DC - 1)
                        if j % 3 == 2:
                            mm.then_inc(l1, 1)

                def layer2(i, r):
                    pe.wait_ge(eo_r, (i * R + r) * B + B)
                    for j in range(HJ):
                        if j % 3 == 0:
                            pe.wait_ge(gelu, (i * R + r) * 2 + j // 3 + 1)
                        mm = pe.matmul(ps[:, 4 + r, 0:D], hid[:, r % 2, j, :], k.w2[r][:, j, :],
                                       start=j == 0, stop=j == HJ - 1)
                    mm.then_inc(l2, 1)

                layer1(0, 0)
                with pe.Fori(0, EC - 1) as i:
                    for r in range(R):
                        layer1(i + (r + 1) // R, (r + 1) % R)
                        layer2(i, r)
                for r in range(R):
                    if r < R - 1:
                        layer1(EC - 1, r + 1)
                    layer2(EC - 1, r)
                pe.wait_ge(eo_r, FREE + EX * B)
                for t in range(TAIL):
                    out = ps[:, t // 2, (t % 2) * D:(t % 2 + 1) * D]
                    col = slice(t * P, (t + 1) * P)
                    for e in range(EC):
                        pe.matmul(out, cwt[:, e, col], eo[:, t // JT, e, :], start=e == 0, stop=False)
                    pe.matmul(out, cst[:, col], k.b2[:, :], start=False, stop=True).then_inc(comb, 1)
                for b in range(B):
                    at = TAIL * P + QUAD * b
                    out = ps[QUAD * b:QUAD * b + 1, 4, 0:D]
                    for e in range(EC):
                        pe.matmul(out, cwt[:, e, at:at + 1], eo[:, b, e, :], start=e == 0, stop=False)
                    pe.matmul(out, cst[:, at:at + 1], k.b2[:, :], start=False, stop=True).then_inc(comb_c, 1)

            @block.scalar
            def _(act):
                with act.Fori(0, EC) as i:
                    for r in range(R):
                        for j in range(HJ):
                            if j % 3 == 0:
                                act.wait_ge(l1, (i * R + r) * 2 + j // 3 + 1)
                            ins = act.activation(
                                hid[:, r % 2, j, :],
                                ps[:, 2 * (r % 2) + j // 3, (j % 3) * P:(j % 3 + 1) * P], ACT.Gelu,
                                bias=k.b1[:, ds(i * R + r, 1), j])
                            if j % 3 == 2:
                                ins.then_inc(gelu, 1)

            @block.vector
            def _(dve):
                dve.sem_inc(eo_r, FREE)
                with dve.Fori(0, EC) as i:
                    for r in range(R):
                        dve.wait_ge(l2, i * R + r + 1)
                        for b in range(B):
                            dve.tensor_copy(
                                eo[SL * r:SL * (r + 1), b, ds(i, 1), :].rearrange("p e d -> p (e d)"),
                                ps[SL * b:SL * (b + 1), 4 + r, 0:D]).then_inc(eo_r, 1)
                for g in range(TAIL // 2):
                    dve.wait_ge(comb, 2 * g + 2)
                    hh = k.h[:, 2 * g:2 * g + 2, :].rearrange("p t d -> p (t d)")
                    dve.tensor_tensor(hh, hh, ps[:, g, 0:2 * D], ALU.add).then_inc(added, 1)
                for b in range(B):
                    dve.wait_ge(comb_c, b + 1)
                    hh = k.h[QUAD * b:QUAD * b + 1, TAIL, :]
                    dve.tensor_tensor(hh, hh, ps[QUAD * b:QUAD * b + 1, 4, 0:D],
                                      ALU.add).then_inc(added, 1)


def layout_soft(i):
    return {
        "phi": i["L0_ffn_phi"].reshape(DC, DK, ES).transpose(1, 0, 2),
        "sscale": i["L0_ffn_scale"].reshape(1, 1),
        "sw1": i["L0_ffn_w1"].reshape(EX, DC, DK, HID).transpose(0, 2, 1, 3),
        "sw2": i["L0_ffn_w2"].reshape(EX, HJ, P, D).transpose(0, 2, 1, 3),
        "sb1": i["L0_ffn_b1"].reshape(EX, HJ, P).transpose(2, 0, 1),
        "sb2": i["L0_ffn_b2"],
    }


NH = 48
CH = 4
UC = 6
HG = 8
NG = NH // HG
BANDW = 2 * P + P + 1
FFT = 2 * L
KC = B * CH * CH
RMS_EPS = 1e-6


def stage_hyena(k, a):
    with ExitStack() as st:
        x0, x1, xv = (k.sb(f"hy_{n}", [P, JT, NH * B * CH], F32, st) for n in ("x0", "x1", "v"))
        x0c, x1c, xvc = (k.sb(f"hy_{n}_cls", [1, NH * B * CH], F32, st) for n in ("x0", "x1", "v"))
        hyena_inputs(k, a, ((x0, x0c), (x1, x1c), (xv, xvc)))
        hyena_mix(k, a, ((x0, x0c), (x1, x1c), (xv, xvc)))


def hyena_inputs(k, a, xs):
    nc, ps = k.nc, k.ps
    with ExitStack() as st:
        def sb(name, shape, dt=F32):
            return k.sb(name, shape, dt, st)

        win = sb("hy_w_in", [DK, DC, 3 * D])
        bin_ = sb("hy_b_in", [DK, UC])
        wsf = sb("hy_w_sf", [DK, UC, 3])
        bsf = sb("hy_b_sf", [DK, UC])
        flip = sb("hy_flip", [P, P])
        xtr = sb("hy_xt_backwards", [DK, DC, TAIL * P])
        uf = sb("hy_u", [DK, 2, B, L + 2])
        ub = sb("hy_u_backwards", [DK, 2, B, L + 2])
        uc = sb("hy_uc", [DK, 2, B, L])
        norm = Norm(k, "hy")
        fl_m, fl_r = k.sem("hy_flipped"), k.sem("hy_flipped_ready")
        w_in, pad, um, ur, c0, c1, c2, tm, xr = (
            k.sem(f"hy_{n}") for n in ("w_loaded", "pads_zero", "u_product", "u_ready", "tap0", "tap1",
                                       "tap2", "turned", "x_ready"))

        with nc.Block() as block:
            @block.sync
            def _(sp):
                for dst, n in ((win[:, :, :], "hwin"), (bin_[:, :], "hbin"), (wsf[:, :, :], "hwsf"),
                               (bsf[:, :], "hbsf"), (flip[:, :], "flip")):
                    sp.dma_start(dst, a[n]).then_inc(w_in, 16)
                if STAGES >= 5:
                    sp.dma_start(k.wi[:, :, :, :], a["wi"]).then_inc(k.s_switch_w, 16)
                    sp.dma_start(k.wo[:, :, :, :], a["wo"]).then_inc(k.s_switch_w, 16)

            @block.gpsimd
            def _(pool):
                pool.memset(uf[:, :, :, 0:2], 0.0).then_inc(pad, 1)
                pool.memset(ub[:, :, :, L:L + 2], 0.0).then_inc(pad, 1)
                norm.gpsimd(pool)

            @block.tensor
            def _(pe):
                norm.tensor(pe)
                pe.wait_ge(w_in, 80)
                for b in range(B):
                    if b == 3:
                        pe.wait_ge(norm.xt_ready, NORM_BANKS)
                    for j in range(JT):
                        for d in range(DC):
                            at = (j * DC + d) * P
                            mm = pe.matmul(ps[0:DK, (5 + b) % 8, at:at + P],
                                           k.xn[:, JT * b + JT - 1 - j, d * DK:(d + 1) * DK],
                                           flip[:, :], start=True, stop=True)
                    mm.then_inc(fl_m, 1)

                def product(q):
                    if q >= 2:
                        pe.wait_ge(ur, 3 * (q - 1))
                        pe.wait_ge(xr, 3 * (q - 1))
                    pe.wait_ge(fl_r, B)
                    src = k.xt if q < 2 else xtr
                    for c in range(3):
                        n = 512 if c < 2 else B
                        for d in range(DC):
                            rhs = (src[:, d, c * 512:(c + 1) * 512] if c < 2
                                   else k.xt[:, d, TAIL * P:NT * P:QUAD])
                            mm = pe.matmul(ps[0:DK, 3 * (q % 2) + c, 0:n],
                                           win[:, d, q * DK:(q + 1) * DK], rhs,
                                           start=d == 0, stop=d == DC - 1)
                        mm.then_inc(um, 1)

                def turn(q):
                    pe.wait_ge(c2, q + 1)
                    if q >= 1:
                        pe.wait_ge(xr, 3 * q)
                    main, cls = (1, 0) if q < 2 else (0, NP_)
                    for j in range(JT):
                        for b in range(B):
                            mm = pe.transpose(ps[:, 6 + j, b * DK:(b + 1) * DK],
                                              uc[:, q % 2, b, main + j * P:main + (j + 1) * P],
                                              k.ident[0:DK, 0:DK])
                    for b in range(B):
                        mm = pe.matmul(ps[0:1, 3 * (q % 2) + 2, P + b * DK:P + (b + 1) * DK],
                                       uc[:, q % 2, b, cls:cls + 1], k.ident[0:DK, 0:DK], start=True, stop=True)
                    mm.then_inc(tm, 1)

                product(0)
                product(1)
                for q in range(UC):
                    turn(q)
                    if q + 2 < UC:
                        product(q + 2)

            @block.scalar
            def _(act):
                norm.scalar(act)
                act.wait_ge(pad, 2)
                for b in range(B):
                    act.wait_ge(fl_m, b + 1)
                    act.activation(
                        xtr[:, :, b * NP_:(b + 1) * NP_].rearrange("p c (t q) -> p t c q", t=JT),
                        ps[0:DK, (5 + b) % 8, :].rearrange("p (t c q) -> p t c q", t=JT, c=DC),
                        ACT.Copy).then_inc(fl_r, 1)

                def bias(q):
                    u, main, cls = (uf, 3, 2) if q < 2 else (ub, 0, NP_)
                    if q >= 2:
                        act.wait_ge(c2, q - 1)
                    for c in range(3):
                        act.wait_ge(um, 3 * q + c + 1)
                        src = ps[0:DK, 3 * (q % 2) + c, 0:512 if c < 2 else B]
                        dst = (u[:, q % 2, 2 * c:2 * c + 2, main:main + NP_] if c < 2
                               else u[:, q % 2, :, cls])
                        if c < 2:
                            src = src.rearrange("p (b l) -> p b l", b=2)
                        act.activation(dst, src, ACT.Identity, bias=bin_[:, q:q + 1]).then_inc(ur, 1)

                bias(0)
                for q in range(UC):
                    if q + 1 < UC:
                        bias(q + 1)
                    x, xc = xs[q // 2]
                    act.wait_ge(tm, q + 1)
                    part = slice((q % 2) * 384, (q % 2 + 1) * 384)
                    for j in range(JT):
                        act.activation(
                            x[:, j, part].rearrange("p (n b i) -> p b n i", b=B, i=CH),
                            ps[:, 6 + j, 0:384].rearrange("p (b n i) -> p b n i", b=B, i=CH),
                            ACT.Copy).then_inc(xr, 1)
                    act.activation(
                        xc[:, part].rearrange("p (n b i) -> p b n i", b=B, i=CH),
                        ps[0:1, 3 * (q % 2) + 2, P:512].rearrange("p (b n i) -> p b n i", b=B, i=CH),
                        ACT.Copy).then_inc(xr, 1)

            @block.vector
            def _(dve):
                norm.vector(dve)
                dve.wait_ge(w_in, 80)
                dve.wait_ge(pad, 2)
                for q in range(UC):
                    dve.wait_ge(ur, 3 * q + 3)
                    if q >= 2:
                        dve.wait_ge(tm, q - 1)
                    o = uc[:, q % 2, :, :]
                    u, at = (uf, (0, 1, 2)) if q < 2 else (ub, (2, 1, 0))
                    dve.tensor_scalar(o, u[:, q % 2, :, at[0]:at[0] + L], wsf[:, q, 0:1], bsf[:, q:q + 1],
                                      ALU.mult, ALU.add).then_inc(c0, 1)
                    dve.wait_ge(c0, q + 1)
                    dve.scalar_tensor_tensor(o, u[:, q % 2, :, at[1]:at[1] + L], wsf[:, q, 1:2], o, ALU.mult,
                                             ALU.add).then_inc(c1, 1)
                    dve.wait_ge(c1, q + 1)
                    dve.scalar_tensor_tensor(o, u[:, q % 2, :, at[2]:at[2] + L], wsf[:, q, 2:3], o, ALU.mult,
                                             ALU.add).then_inc(c2, 1)


def hyena_mix(k, a, xs):
    nc, ps = k.nc, k.ps
    (x0, x0c), (x1, x1c), (xv, xvc) = xs
    GN = HG * B
    with ExitStack() as st:
        def sb(name, shape, dt=F32):
            return k.sb(name, shape, dt, st)

        band = sb("hy_band", [P, 2, HG, BANDW])
        first = sb("hy_first", [1, 2, HG, L])
        kv = sb("hy_kv", [P, 2, JT, HG * KC])
        kvc = sb("hy_kv_cls", [1, 2, HG * KC])
        prod = sb("hy_prod", [P, 3, HG * KC])
        y = sb("hy_y", [P, NT, D])
        yc = sb("hy_y_cls", [1, B, D])
        yt = k.xt
        wout = sb("hy_w_out", [DK, DC, D])
        bout = sb("hy_b_out", [1, D])
        nw = sb("hy_norm_w", [DK, DC])
        ms = sb("hy_ms", [P, NT])
        mse = sb("hy_mse", [P, NT])
        rms = sb("hy_rms", [P, NT])
        w_in, kv_r, conv, gated, summed, cls_zero, cls_moved = (
            k.sem(f"hy_{n}") for n in ("w2_loaded", "kv_ready", "conv", "gated", "summed",
                                       "cls_zero", "cls_moved"))
        band_in = [k.sem(f"hy_band_loaded{r}") for r in range(2)]
        ms_r, mse_r, rms_r, yn_r, yn_t, yt_r, proj, h1, h2 = (
            k.sem(f"hy_{n}") for n in ("ms", "mse", "rms", "y_scaled", "y_turned", "yt_ready", "proj",
                                       "h_plus_x", "h_added"))
        EXT = FFT - 1

        with nc.Block() as block:
            @block.sync
            def _(sp):
                for g in range(NG):
                    if g >= 2:
                        sp.wait_ge(conv, 3 * (g - 1))
                    ext = a["hext"]
                    sp.dma_start(band[:, g % 2, :, :],
                                 bass.AP(tensor=ext.tensor, offset=g * HG * EXT,
                                         ap=[[1, P], [EXT, HG], [1, BANDW]])).then_inc(band_in[g % 2], 16)
                    sp.dma_start(first[:, g % 2, :, :],
                                 a["hh"][:, g * HG:(g + 1) * HG, 0:L]).then_inc(band_in[g % 2], 16)
                    if g == 1:
                        for dst, n in ((wout[:, :, :], "hwout"), (bout[:, :], "hbout"), (nw[:, :], "hnw")):
                            sp.dma_start(dst, a[n]).then_inc(w_in, 16)
                sp.wait_ge(summed, 3 * NG)
                sp.wait_ge(cls_zero, 1)
                for b in range(B):
                    sp.dma_start(y[QUAD * b:QUAD * b + 1, TAIL, :], yc[:, b, :]).then_inc(cls_moved, 16)

            @block.gpsimd
            def _(pool):
                pool.memset(y[:, TAIL, :], 0.0).then_inc(cls_zero, 1)
                for g in range(NG):
                    if g >= 2:
                        pool.wait_ge(conv, 3 * (g - 1))
                    part = slice(g * GN * CH, (g + 1) * GN * CH)

                    def outer(dst, p, q):
                        pool.tensor_tensor(
                            dst.rearrange("p (n i j) -> p n i j", i=CH, j=CH),
                            bc(p.rearrange("p (n i) -> p n i", i=CH), 3, CH),
                            bc(q.rearrange("p (n j) -> p n j", j=CH), 2, CH), ALU.mult).then_inc(kv_r, 1)

                    for s in range(JT):
                        outer(kv[:, g % 2, s, :], x1[:, s, part], xv[:, s, part])
                    outer(kvc[:, g % 2, :], x1c[:, part], xvc[:, part])
                pool.wait_ge(mse_r, 1)
                pool.tensor_tensor(rms[:, :], mse[:, :], k.half[:, :], ALU.pow).then_inc(rms_r, 1)

            @block.tensor
            def _(pe):
                for g in range(NG):
                    r = g % 2
                    pe.wait_ge(band_in[r], 32 * (g // 2 + 1))
                    pe.wait_ge(kv_r, 3 * (g + 1))
                    if g >= 2:
                        pe.wait_ge(gated, 3 * (g - 1))
                    for t in range(JT + 1):
                        for n in range(HG):
                            col = slice(n * KC, (n + 1) * KC)
                            if t < JT:
                                out = ps[:, 3 * r + t, col]
                                lhs = [band[:, r, n, P * (t + s) + 1:P * (t + s + 1) + 1]
                                       for s in range(JT)]
                                own = first[:, r, n, 1 + t * P:1 + (t + 1) * P]
                            else:
                                out = ps[0:1, 3 * r + t, col]
                                lhs = [band[:, r, n, P * s:P * s + 1] for s in range(JT)]
                                own = first[:, r, n, 0:1]
                            for s in range(JT):
                                pe.matmul(out, lhs[s], kv[:, r, s, col], start=s == 0, stop=False)
                            mm = pe.matmul(out, own, kvc[:, r, col], start=False, stop=True)
                        mm.then_inc(conv, 1)
                pe.wait_ge(gated, 3 * NG)
                for t in range(NT):
                    pe.wait_ge(yn_r, t + 1)
                    for d in range(DC):
                        at = (t % 2) * 2 * P + d * P
                        mm = pe.transpose(ps[0:DK, t // 2, at:at + P], y[:, t, d * DK:(d + 1) * DK],
                                          k.ident[:, :])
                    mm.then_inc(yn_t, 1)
                pe.wait_ge(w_in, 48)
                for t in range(NT):
                    pe.wait_ge(yt_r, 2 * (t // 2) + 2)
                    if t >= 6 and t % 2 == 0:
                        pe.wait_ge(h2, t // 2 - 2)
                    out = ps[:, 5 + t // 2 % 3, (t % 2) * D:(t % 2 + 1) * D]
                    for d in range(DC):
                        pe.matmul(out, yt[:, d, t * P:(t + 1) * P], wout[:, d, :], start=d == 0, stop=False)
                    pe.matmul(out, k.ones[0:1, :], bout[:, :], start=False, stop=True).then_inc(proj, 1)

            @block.scalar
            def _(act):
                for t in range(NT):
                    act.wait_ge(summed, 3 * NG)
                    if t == TAIL:
                        act.wait_ge(cls_moved, 16 * B)
                    if t >= 1:
                        act.wait_ge(ms_r, t)
                    act.activation(prod[:, 0, 0:D], y[:, t, :], ACT.Square,
                                   accum_out=ms[:, t:t + 1]).then_inc(ms_r, 1)
                act.wait_ge(w_in, 48)
                for g in range(NORM_BANKS):
                    n = min(2, NT - 2 * g)
                    act.wait_ge(yn_t, 2 * g + n)
                    for d in range(DC):
                        act.activation(
                            yt[:, d, 2 * g * P:(2 * g + n) * P].rearrange("p (t q) -> p t q", t=n),
                            ps[0:DK, g, 0:2 * n * P].rearrange("p (t c q) -> p t c q", t=n, c=DC)[:, :, d, :],
                            ACT.Copy, scale=nw[:, d:d + 1]).then_inc(yt_r, 1)

            @block.vector
            def _(dve):
                for g in range(NG):
                    r = g % 2
                    part = slice(g * GN * CH, (g + 1) * GN * CH)
                    for t in range(JT + 1):
                        rows = slice(0, P if t < JT else 1)
                        x = x0[:, t, part] if t < JT else x0c[:, part]
                        pr = prod[rows, t, :]
                        dve.wait_ge(conv, 3 * g + t + 1)
                        dve.tensor_tensor(pr.rearrange("p (n j) -> p n j", j=CH),
                                          ps[rows, 3 * r + t, :].rearrange("p (n j) -> p n j", j=CH),
                                          bc(x, 2, CH), ALU.mult).then_inc(gated, 1)
                        dve.wait_ge(gated, 3 * g + t + 1)
                        if t < JT:
                            dst = y[:, t:TAIL:JT, g * HG * CH:(g + 1) * HG * CH]
                        else:
                            dst = yc[:, :, g * HG * CH:(g + 1) * HG * CH]
                        dve.tensor_reduce(dst.rearrange("p b (n j) -> p n b j", j=CH),
                                          pr.rearrange("p (n b i j) -> p n b j i", b=B, i=CH, j=CH),
                                          AXX, ALU.add).then_inc(summed, 1)
                dve.wait_ge(ms_r, NT)
                dve.tensor_scalar(mse[:, :], ms[:, :], 1.0 / D, RMS_EPS, ALU.mult, ALU.add).then_inc(mse_r, 1)
                dve.wait_ge(rms_r, 1)
                for t in range(NT):
                    dve.tensor_scalar(y[:, t, :], y[:, t, :], rms[:, t:t + 1], None,
                                      ALU.mult).then_inc(yn_r, 1)
                dve.tensor_tensor(k.h[:, :, :], k.h[:, :, :], k.xn[:, :, :], ALU.add).then_inc(h1, 1)
                dve.wait_ge(h1, 1)
                for g in range(NORM_BANKS):
                    n = min(2, NT - 2 * g)
                    dve.wait_ge(proj, 2 * g + n)
                    hh = k.h[:, 2 * g:2 * g + n, :].rearrange("p t d -> p (t d)")
                    dve.tensor_tensor(hh, hh, ps[:, 5 + g % 3, 0:n * D], ALU.add).then_inc(h2, 1)


def layout_hyena(i):
    import numpy as np

    def by_type(w):
        return w.reshape(NH, 3, CH, -1).transpose(1, 0, 2, 3).reshape(3 * D, -1)

    h = i["L1_attn_h"]
    ring = np.concatenate([h, np.zeros((NH, FFT - h.shape[1]), np.float32)], 1)
    return {
        "flip": np.eye(P, dtype=np.float32)[::-1],
        "hwin": by_type(i["L1_attn_w_in"]).T.reshape(DC, DK, 3 * D).transpose(1, 0, 2),
        "hbin": by_type(i["L1_attn_b_in"]).reshape(UC, DK).T,
        "hwsf": by_type(i["L1_attn_w_sf"]).reshape(UC, DK, 3).transpose(1, 0, 2),
        "hbsf": by_type(i["L1_attn_b_sf"]).reshape(UC, DK).T,
        "hext": np.concatenate([ring[:, L + 1:], ring[:, :L]], 1),
        "hh": ring.reshape(1, NH, FFT),
        "hwout": i["L1_attn_w_out"].T.reshape(DC, DK, D).transpose(1, 0, 2),
        "hbout": i["L1_attn_b_out"].reshape(1, D),
        "hnw": i["L1_attn_norm_w"].reshape(DC, DK).T,
    }


SE = 8
ST = (B * L + SE * (P - 1)) // P
RING = 3
TURNS = ST // RING
TOKEN_TILES = -(-B * L // P)
HH = HID // 2


def alloc_switch(k, a, st):
    k.wi = k.sb("switch_wi", [DK, SE, DC, HID], F32, st)
    k.wo = k.sb("switch_wo", [P, SE, HJ, D], F32, st)
    k.s_switch_w = k.sem("switch_weights_loaded")
    k.sorted_x = k.nc.dram_tensor("sorted_x", ((ST + 1) * P, D), F32, kind="Internal").ap()
    k.sorted_y = k.nc.dram_tensor("sorted_y", ((ST + 1) * P, D), F32, kind="Internal").ap()


def stage_switch(k, a):
    nc, ps = k.nc, k.ps
    with ExitStack() as st:
        def sb(name, shape, dt=F32):
            return k.sb(name, shape, dt, st)

        rw = sb("router_w", [DK, DC, SE])
        tri = sb("before", [P, P])
        desc = sb("descending", [P, NT, SE])
        steps = sb("tile_steps", [P, SE, TOKEN_TILES])
        lower = sb("lower", [P, SE, SE])
        valid = sb("valid", [P, NT])
        spare = sb("spare", [P, NT])
        tile_no = sb("tile_no", [1, ST, SE])
        zeros = sb("zeros", [P, D])
        lm = sb("lm", [P, NT])
        sh = sb("sh", [P, NT, SE])
        pe_ = sb("pexp", [P, NT, SE])
        psum_ = sb("prob_sum", [P, NT])
        top = sb("top_prob", [P, NT])
        eq = sb("eq", [P, NT, SE])
        first = sb("first_max", [P, NT])
        oh = sb("one_hot", [P, NT + 1, SE])
        many = sb("many", [P, SE, TOKEN_TILES])
        tiles_of = sb("tiles_of", [P, SE])
        bl = sb("base_terms", [P, SE, SE])
        base = sb("base", [P, SE])
        end = sb("end", [P, SE])
        place = sb("place", [P, NT, SE])
        dest = sb("dest", [P, NT])
        desti = sb("dest_rows", [P, NT], I32)
        te = sb("tile_terms", [1, ST, SE])
        tef = sb("tile_expert_f", [1, ST])
        tei = sb("tile_expert", [1, ST], I32)
        xs = [sb(f"tile_x{r}", [P, D]) for r in range(RING)]
        xst = sb("tile_xt", [DK, DC, P])
        hs = sb("tile_h", [P, HID])
        hst = sb("tile_ht", [P, HJ, P])
        ys = [sb(f"tile_y{r}", [P, D]) for r in range(RING)]
        yg = sb("token_y", [P, NT, D])

        norm = Norm(k, "switch")
        c_in, zero, cleared = (k.sem(f"switch_{n}") for n in ("consts_loaded", "zeros_ready", "scratch_clear"))
        lg, rank = k.sem("switch_logits"), k.sem("switch_ranks")
        step = k.sem("switch_routing_step")
        pexp = k.sem("switch_exp")
        oh_r, dest_r, te_r = (k.sem(f"switch_{n}") for n in ("one_hot", "dest", "tile_expert"))
        scattered, stored, gathered = (k.sem(f"switch_{n}") for n in ("scattered", "stored", "gathered"))
        xs_in = [k.sem(f"switch_tile_loaded{r}") for r in range(RING)]
        ys_out = [k.sem(f"switch_tile_stored{r}") for r in range(RING)]
        xt_m, xt_r, h_m, h_a, h_v, ht_m, ht_a, ht_v, y_m, y_r, added = (
            k.sem(f"switch_{n}") for n in ("x_turned", "xt_ready", "layer1", "relu_left", "relu_right",
                                           "h_turned", "ht_left", "ht_right", "layer2", "y_ready", "added"))
        consts = ((rw[:, :, :], "rw"), (tri[:, :], "before"), (desc[:, :, :], "desc"),
                  (steps[:, :, :], "steps"), (lower[:, :, :], "lower"), (valid[:, :], "valid"),
                  (spare[:, :], "spare"), (tile_no[:, :, :], "tile_no"))
        N_CLEAR = ST + 2

        with nc.Block() as block:
            @block.sync
            def _(sp):
                for dst, n in consts:
                    sp.dma_start(dst, a[n]).then_inc(c_in, 16)
                sp.wait_ge(zero, 1)
                for t in range(ST + 1):
                    sp.dma_start(k.sorted_x[t * P:(t + 1) * P, :], zeros[:, :]).then_inc(cleared, 16)
                sp.dma_start(k.sorted_y[ST * P:(ST + 1) * P, :], zeros[:, :]).then_inc(cleared, 16)
                sp.wait_ge(scattered, 16 * NT)
                for r in range(RING):
                    sp.dma_start(xs[r][:, :], k.sorted_x[r * P:(r + 1) * P, :]).then_inc(xs_in[r], 16)
                with sp.Fori(1, TURNS) as i:
                    for r in range(RING):
                        sp.wait_ge(xt_m, (i - 1) * RING + r + 1)
                        sp.dma_start(xs[r][:, :], k.sorted_x[ds((i * RING + r) * P, P), :]).then_inc(xs_in[r], 16)

            @block.gpsimd
            def _(pool):
                pool.memset(zeros[:, :], 0.0).then_inc(zero, 1)
                pool.memset(oh[:, NT, :], 0.0).then_inc(zero, 1)
                norm.gpsimd(pool)
                pool.wait_ge(cleared, 16 * N_CLEAR)
                pool.wait_ge(dest_r, 1)
                for t in range(NT):
                    pool.indirect_dma_start(k.sorted_x, bass.IndirectOffsetOnAxis(ap=desti[:, t:t + 1], axis=0),
                                            k.xn[:, t, :], None).then_inc(scattered, 16)
                with pool.Fori(0, TURNS) as i:
                    for r in range(RING):
                        pool.wait_ge(y_r, i * RING + r + 1)
                        pool.dma_start(k.sorted_y[ds((i * RING + r) * P, P), :], ys[r][:, :]).then_inc(ys_out[r], 16)
                for r in range(RING):
                    pool.wait_ge(ys_out[r], 16 * TURNS)
                for t in range(NT):
                    pool.indirect_dma_start(yg[:, t, :], None, k.sorted_y,
                                            bass.IndirectOffsetOnAxis(ap=desti[:, t:t + 1], axis=0)
                                            ).then_inc(gathered, 16)

            @block.tensor
            def _(pe):
                norm.tensor(pe)
                pe.wait_ge(c_in, 16 * len(consts))
                pe.wait_ge(norm.xt_ready, NORM_BANKS)
                for t in range(NT):
                    for d in range(DC):
                        mm = pe.matmul(ps[:, 5, t * SE:(t + 1) * SE], k.xt[:, d, t * P:(t + 1) * P],
                                       rw[:, d, :], start=d == 0, stop=d == DC - 1)
                mm.then_inc(lg, 1)
                pe.wait_ge(oh_r, 1)
                pe.wait_ge(zero, 2)
                cols = (NT + 1) * SE
                pe.matmul(ps[:, 6, 0:cols], tri[:, :], oh[:, :, :].rearrange("p t e -> p (t e)"),
                          start=True, stop=False)
                for t in range(NT):
                    n = NT - t
                    mm = pe.matmul(ps[:, 6, (t + 1) * SE:cols].rearrange("p (t e) -> p t e", t=n),
                                   k.ones[:, :], oh[:, t:t + 1, :].broadcast_to([P, n, SE]),
                                   start=False, stop=t == NT - 1)
                mm.then_inc(rank, 1)

                pe.wait_ge(te_r, 1)
                pe.wait_ge(k.s_switch_w, 32)

                def expert_of(t):
                    return pe.value_load(tei[0:1, ds(t, 1)], min_val=0, max_val=SE - 1)

                def turn_x(i, r):
                    pe.wait_ge(xs_in[r], i * 16 + 16)
                    for d in range(DC):
                        mm = pe.transpose(ps[0:DK, 0, d * P:(d + 1) * P], xs[r][:, d * DK:(d + 1) * DK],
                                          k.ident[:, :])
                    mm.then_inc(xt_m, 1)

                def layer1(i, r):
                    e = expert_of(i * RING + r)
                    pe.wait_ge(xt_r, i * RING + r + 1)
                    for c in range(2):
                        for d in range(DC):
                            mm = pe.matmul(ps[:, 1 + c, 0:HH], xst[:, d, :],
                                           k.wi[:, ds(e, 1), d, c * HH:(c + 1) * HH].rearrange(
                                               "p e n -> p (e n)"), start=d == 0, stop=d == DC - 1)
                        mm.then_inc(h_m, 1)

                def turn_h(i, r):
                    pe.wait_ge(h_a, i * RING + r + 1)
                    pe.wait_ge(h_v, i * RING + r + 1)
                    for j in range(HJ):
                        mm = pe.transpose(ps[:, 3 + j // 3, (j % 3) * P:(j % 3 + 1) * P],
                                          hs[:, j * P:(j + 1) * P], k.ident[:, :])
                    mm.then_inc(ht_m, 1)

                def layer2(i, r):
                    e = expert_of(i * RING + r)
                    pe.wait_ge(ht_a, i * RING + r + 1)
                    pe.wait_ge(ht_v, i * RING + r + 1)
                    for j in range(HJ):
                        mm = pe.matmul(ps[:, 5 + r, 0:D], hst[:, j, :],
                                       k.wo[:, ds(e, 1), j, :].rearrange("p e n -> p (e n)"),
                                       start=j == 0, stop=j == HJ - 1)
                    mm.then_inc(y_m, 1)

                turn_x(0, 0)
                layer1(0, 0)
                with pe.Fori(0, TURNS - 1) as i:
                    for r in range(RING):
                        nxt = (i + (r + 1) // RING, (r + 1) % RING)
                        turn_x(*nxt)
                        turn_h(i, r)
                        layer1(*nxt)
                        layer2(i, r)
                for r in range(RING):
                    if r < RING - 1:
                        turn_x(TURNS - 1, r + 1)
                    turn_h(TURNS - 1, r)
                    if r < RING - 1:
                        layer1(TURNS - 1, r + 1)
                    layer2(TURNS - 1, r)

            @block.scalar
            def _(act):
                norm.scalar(act)
                act.wait_ge(step, 2)
                act.activation(pe_[:, :, :], sh[:, :, :], ACT.Exp).then_inc(pexp, 1)

                def xt_copy(t):
                    act.wait_ge(xt_m, t + 1)
                    act.activation(xst[:, :, :].rearrange("p c q -> p (c q)"), ps[0:DK, 0, 0:DC * P],
                                   ACT.Copy).then_inc(xt_r, 1)

                def relu(t):
                    act.wait_ge(h_m, 2 * t + 1)
                    act.activation(hs[:, 0:HH], ps[:, 1, 0:HH], ACT.Relu).then_inc(h_a, 1)

                def ht_copy(t):
                    act.wait_ge(ht_m, t + 1)
                    act.activation(hst[:, 0:3, :].rearrange("p j q -> p (j q)"), ps[:, 3, 0:HH],
                                   ACT.Copy).then_inc(ht_a, 1)

                xt_copy(0)
                relu(0)
                with act.Fori(1, ST) as t:
                    xt_copy(t)
                    ht_copy(t - 1)
                    relu(t)
                ht_copy(ST - 1)

            @block.vector
            def _(dve):
                norm.vector(dve)
                n_step = 0

                def routed(ins):
                    nonlocal n_step
                    n_step += 1
                    ins.then_inc(step, 1)
                    dve.wait_ge(step, n_step)

                dve.wait_ge(lg, 1)
                dve.wait_ge(c_in, 16 * len(consts))
                logits = ps[:, 5, 0:NT * SE].rearrange("p (t e) -> p t e", t=NT)
                routed(dve.tensor_reduce(lm[:, :], logits, AXX, ALU.max))
                routed(dve.tensor_tensor(sh[:, :, :], logits, bc(lm[:, :], 2, SE), ALU.subtract))
                routed(dve.tensor_tensor(eq[:, :, :], logits, bc(lm[:, :], 2, SE), ALU.is_equal))
                routed(dve.tensor_tensor(eq[:, :, :], eq[:, :, :], desc[:, :, :], ALU.mult))
                routed(dve.tensor_reduce(first[:, :], eq[:, :, :], AXX, ALU.max))
                routed(dve.tensor_tensor(eq[:, :, :], eq[:, :, :], bc(first[:, :], 2, SE), ALU.is_equal))
                dve.tensor_tensor(oh[:, 0:NT, :], eq[:, :, :], bc(valid[:, :], 2, SE),
                                  ALU.mult).then_inc(oh_r, 1)
                dve.wait_ge(pexp, 1)
                routed(dve.tensor_reduce(psum_[:, :], pe_[:, :, :], AXX, ALU.add))
                routed(dve.reciprocal(top[:, :], psum_[:, :]))
                dve.wait_ge(rank, 1)
                dve.wait_ge(oh_r, 1)
                total = ps[:, 6, NT * SE:(NT + 1) * SE]
                routed(dve.tensor_tensor(many[:, :, :], bc(total, 2, TOKEN_TILES), steps[:, :, :], ALU.is_gt))
                routed(dve.tensor_reduce(tiles_of[:, :], many[:, :, :], AXX, ALU.add))
                routed(dve.tensor_tensor(bl[:, :, :], bc(tiles_of[:, :], 1, SE), lower[:, :, :], ALU.mult))
                routed(dve.tensor_reduce(base[:, :], bl[:, :, :], AXX, ALU.add))
                routed(dve.tensor_tensor(end[:, :], base[:, :], tiles_of[:, :], ALU.add))
                routed(dve.tensor_scalar(base[:, :], base[:, :], float(P), None, ALU.mult))
                routed(dve.tensor_tensor(place[:, :, :],
                                         ps[:, 6, 0:NT * SE].rearrange("p (t e) -> p t e", t=NT),
                                         bc(base[:, :], 1, NT), ALU.add))
                routed(dve.tensor_tensor(place[:, :, :], place[:, :, :], oh[:, 0:NT, :], ALU.mult))
                routed(dve.tensor_reduce(dest[:, :], place[:, :, :], AXX, ALU.add))
                dve.tensor_tensor(desti[:, :], dest[:, :], spare[:, :], ALU.add).then_inc(dest_r, 1)
                routed(dve.tensor_tensor(te[:, :, :], tile_no[:, :, :], bc(end[0:1, :], 1, ST), ALU.is_ge))
                routed(dve.tensor_reduce(tef[:, :], te[:, :, :], AXX, ALU.add))
                dve.tensor_scalar(tei[:, :], tef[:, :], float(SE - 1), None, ALU.min).then_inc(te_r, 1)

                def relu(t):
                    dve.wait_ge(h_m, 2 * t + 2)
                    dve.tensor_scalar(hs[:, HH:HID], ps[:, 2, 0:HH], 0.0, None, ALU.max).then_inc(h_v, 1)

                def ht_copy(t):
                    dve.wait_ge(ht_m, t + 1)
                    dve.tensor_copy(hst[:, 3:6, :].rearrange("p j q -> p (j q)"),
                                    ps[:, 4, 0:HH]).then_inc(ht_v, 1)

                def y_copy(i, r):
                    dve.wait_ge(y_m, i * RING + r + 1)
                    dve.tensor_copy(ys[r][:, :], ps[:, 5 + r, 0:D]).then_inc(y_r, 1)

                def tile(i, r):
                    t = i * RING + r
                    ht_copy(t)
                    relu(t + 1)
                    y_copy(i, r)

                relu(0)
                for r in range(RING):
                    tile(0, r)
                with dve.Fori(1, TURNS - 1) as i:
                    for r in range(RING):
                        dve.wait_ge(ys_out[r], i * 16)
                        tile(i, r)
                for r in range(RING):
                    dve.wait_ge(ys_out[r], 16 * (TURNS - 1))
                    if r < RING - 1:
                        tile(TURNS - 1, r)
                ht_copy(ST - 1)
                y_copy(TURNS - 1, RING - 1)
                for t in range(NT):
                    dve.wait_ge(gathered, 16 * NT)
                    dve.scalar_tensor_tensor(k.h[:, t, :], yg[:, t, :], top[:, t:t + 1], k.h[:, t, :],
                                             ALU.mult, ALU.add).then_inc(added, 1)


def layout_switch(i):
    import numpy as np

    one = np.ones
    valid = one((P, NT), np.float32)
    valid[:, TAIL] = 0
    valid[QUAD * np.arange(B), TAIL] = 1
    spare = np.where(valid > 0, 0, ST * P + np.arange(P)[:, None]).astype(np.float32)
    e = np.arange(SE)
    f = np.float32
    return {
        "rw": i["L1_ffn_router_w"].reshape(DC, DK, SE).transpose(1, 0, 2),
        "wi": i["L1_ffn_wi"].reshape(SE, DC, DK, HID).transpose(2, 0, 1, 3),
        "wo": i["L1_ffn_wo"].reshape(SE, HJ, P, D).transpose(2, 0, 1, 3),
        "before": np.triu(one((P, P), f), 1),
        "desc": np.broadcast_to((SE - e).astype(f), (P, NT, SE)),
        "steps": np.broadcast_to((P * np.arange(TOKEN_TILES)).astype(f), (P, SE, TOKEN_TILES)),
        "lower": np.broadcast_to((e[:, None] > e[None, :]).astype(f), (P, SE, SE)),
        "valid": valid,
        "spare": spare,
        "tile_no": np.broadcast_to(np.arange(ST).astype(f)[None, :, None], (1, ST, SE)),
    }


def run(k, stage, *args):
    k.in_stage = True
    stage(k, *args)
    k.in_stage = False
    k.nc.clear_and_free_semaphores(k.stage_sems)
    k.nc.all_engine_barrier()
    k.stage_sems = []


def build(nc, a, out):
    with ExitStack() as ctx:
        k = Core(nc, ctx)
        with ExitStack() as first_layer:
            if STAGES >= 3:
                alloc_soft(k, a, first_layer)
            with ExitStack() as attention:
                if STAGES >= 2:
                    alloc_attn(k, a, attention)
                run(k, stage_tok, a)
                if STAGES >= 2:
                    run(k, stage_attn, a)
            if STAGES >= 3:
                run(k, stage_soft, a)
        if STAGES >= 4:
            if STAGES >= 5:
                alloc_switch(k, a, ctx)
            run(k, stage_hyena, a)
        if STAGES >= 5:
            run(k, stage_switch, a)
        run(k, store, out)


def upsample(n_in, n_out):
    import numpy as np

    pos = (np.arange(n_out, dtype=np.float32) + np.float32(0.5)) * np.float32(n_in / n_out) - np.float32(0.5)
    pos = np.clip(pos, 0.0, n_in - 1).astype(np.float32)
    i0 = np.floor(pos).astype(np.int32)
    w = (pos - i0).astype(np.float32)
    m = np.zeros((n_in, n_out), np.float32)
    np.add.at(m, (i0, np.arange(n_out)), np.float32(1) - w)
    np.add.at(m, (np.minimum(i0 + 1, n_in - 1), np.arange(n_out)), w)
    return m


def layout(i):
    import numpy as np

    x = i["x"]
    o = {
        "x0": x.transpose(2, 3, 0, 1).reshape(4096, 12),
        "x1": x.reshape(4, 3, 32, 2, 32, 2).transpose(2, 4, 0, 3, 5, 1).reshape(1024, 48),
        "x2": x.reshape(4, 3, 16, 4, 16, 4).transpose(2, 4, 0, 3, 5, 1).reshape(256, 192),
        "idx0": i["L0_tok_idx0"].reshape(2, 128, 16).transpose(1, 0, 2).reshape(128, 32),
        "idx1": i["L0_tok_idx1"].reshape(64, 2, 8).transpose(1, 0, 2).reshape(128, 8),
        "idx2": i["L0_tok_idx2"].reshape(16, 2, 8).transpose(2, 0, 1).reshape(128, 2),
        "tw0": i["L0_tok_W0"].T,
        "tw1": i["L0_tok_W1"].T.reshape(2, 96, 64).transpose(1, 0, 2),
        "tw2": i["L0_tok_W2"].T.reshape(16, 48, 64).transpose(1, 0, 2),
        "tb": np.stack([i["L0_tok_b0"], i["L0_tok_b1"], i["L0_tok_b2"]], 1),
        "twf": i["L0_tok_Wf"].T.reshape(3, 64, 192).transpose(1, 0, 2),
        "tbf": i["L0_tok_bf"].reshape(1, 192),
        "cls": i["cls_tok"].reshape(1, 192),
        "ident": np.eye(128, dtype=np.float32),
        "up1": np.concatenate([upsample(64, 256), np.ones((1, 256), np.float32)]),
        "up2": upsample(16, 256),
    }
    for f in (layout_attn, layout_soft, layout_hyena, layout_switch):
        o.update(f(i))
    return {n: np.ascontiguousarray(v) for n, v in o.items()}


def kernel(**inputs):
    import numpy as np
    import concourse.bacc as bacc
    from concourse.bass_utils import run_bass_kernel_spmd

    arrays = layout({n: np.asarray(v) for n, v in inputs.items()})
    nc = bacc.Bacc("TRN2", target_bir_lowering=False, num_devices=1)
    a = {n: nc.dram_tensor(f"in_{n}", v.shape, mybir.dt.from_np(v.dtype), kind="ExternalInput").ap()
         for n, v in arrays.items()}
    out = nc.dram_tensor("out_0", (B, L, D), F32, kind="ExternalOutput").ap()
    build(nc, a, out)
    r = run_bass_kernel_spmd(nc, [{f"in_{n}": v for n, v in arrays.items()}], core_ids=[0])
    return r.results[0]["out_0"]
```
